# Optimizing a Trainium2 kernel written in Bass

```python
import numpy as np
import jax
import jax.numpy as jnp

def _softmax(x, axis=-1):
    return jax.nn.softmax(x, axis=axis)
def _gelu(x):
    return jax.nn.gelu(x, approximate=True)
def _silu(x):
    return jax.nn.silu(x)
def _sigmoid(x):
    return jax.nn.sigmoid(x)
def _layernorm(x, axis=-1, eps=1e-5):
    m = jnp.mean(x, axis=axis, keepdims=True)
    v = jnp.var(x, axis=axis, keepdims=True)
    return (x - m) / jnp.sqrt(v + eps)
def _scatter_add(tgt, idx, src, axis=0):
    return tgt.at[idx].add(src)
def _segment_sum(src, seg, n):
    return jax.ops.segment_sum(src, seg, n)

kernel_name = 'mk_conv_preact_d2_conv_nchw128_720ce3'

def setup_inputs(seed: int = 0):
    np.random.seed(seed)
    _w = jnp.asarray
    def _rec_inputs():
        import jax
        import jax.numpy as jnp
        _gk = jax.random.key(seed)
        x = 7.22e-05 + 1 * jax.random.normal(jax.random.fold_in(_gk, 1), (4, 128, 128, 128), jnp.float32)
        return x
    x = _rec_inputs()
    def _L0_conv_setup():
        import jax, jax.numpy as jnp
        import numpy as np
        DIM = 128
        HID = 4 * DIM
        EPS = 1e-05

        def _ln(x, g, b):
            mu = jnp.mean(x, axis=-1, keepdims=True)
            var = jnp.mean(jnp.square(x - mu), axis=-1, keepdims=True)
            return (x - mu) * jax.lax.rsqrt(var + EPS) * g + b

        def _block(x, ln0_g, ln0_b, ln1_g, ln1_b, ln2_g, ln2_b, W_out, W_whiten, W_key, W_recep, W_value):
            b, c, h, w = x.shape
            t = x.reshape(b, c, h * w).transpose(0, 2, 1)
            t = _ln(t, ln0_g, ln0_b)
            y1 = _ln(t, ln1_g, ln1_b)
            att = jnp.einsum('btc,oc->bto', jax.nn.sigmoid(y1) * y1, W_out)
            t = t + att
            y2 = _ln(t, ln2_g, ln2_b)
            wht = jnp.einsum('btc,oc->bto', y2, W_whiten)
            k = jnp.square(jax.nn.relu(jnp.einsum('btc,hc->bth', wht, W_key)))
            kv = jnp.einsum('bth,ch->btc', k, W_value)
            r = jax.nn.sigmoid(jnp.einsum('btc,oc->bto', wht, W_recep))
            t = t + r * kv
            return t.transpose(0, 2, 1).reshape(b, c, h, w)
        key = jax.random.key(seed)
        ks = jax.random.split(key, 8)
        b, c, h, w = (4, DIM, 128, 128)
        inp = {'inp_img': jax.random.normal(ks[0], (b, c, h, w), dtype=jnp.float32), 'ln0_g': jnp.ones((c,), jnp.float32), 'ln0_b': jnp.zeros((c,), jnp.float32), 'ln1_g': jnp.ones((c,), jnp.float32), 'ln1_b': jnp.zeros((c,), jnp.float32), 'ln2_g': jnp.ones((c,), jnp.float32), 'ln2_b': jnp.zeros((c,), jnp.float32), 'W_out': jax.random.normal(ks[1], (c, c), jnp.float32) * 0.05, 'W_whiten': jax.random.normal(ks[2], (c, c), jnp.float32) * 0.05, 'W_key': jax.random.normal(ks[3], (HID, c), jnp.float32) * 0.05, 'W_recep': jax.random.normal(ks[4], (c, c), jnp.float32) * 0.05, 'W_value': jax.random.normal(ks[5], (c, HID), jnp.float32) * 0.05}
        return inp
    _L0_conv_all = _L0_conv_setup()
    _L0_conv_in = {k: v for k, v in _L0_conv_all.items() if k in ('ln0_g', 'ln0_b', 'ln1_g', 'ln1_b', 'ln2_g', 'ln2_b', 'W_out', 'W_whiten', 'W_key', 'W_recep', 'W_value', )}
    del _L0_conv_all

    def _L1_conv_setup():
        import jax, jax.numpy as jnp
        import numpy as np
        BS, C, H, W = (4, 128, 64, 64)
        IC = C // 2
        key = jax.random.key(seed)
        k0, k1, k2, k3, k4, k5 = jax.random.split(key, 6)
        s_in = 1.0 / np.sqrt(C)
        s_ic = 1.0 / np.sqrt(IC)
        return {'x': jax.random.normal(k0, (BS, C, H, W), dtype=jnp.float32), 'Wq': jax.random.normal(k1, (IC, C), dtype=jnp.float32) * s_in, 'Wk': jax.random.normal(k2, (IC, C), dtype=jnp.float32) * s_in, 'Wv': jax.random.normal(k3, (IC, C), dtype=jnp.float32) * s_in, 'B': jax.random.normal(k4, (IC, IC), dtype=jnp.float32) * 0.02, 'Wm': jax.random.normal(k5, (C, IC), dtype=jnp.float32) * s_ic}
    _L1_conv_all = _L1_conv_setup()
    _L1_conv_in = {k: v for k, v in _L1_conv_all.items() if k in ('Wq', 'Wk', 'Wv', 'B', 'Wm', )}
    del _L1_conv_all

    return {
        "x": x,
        "L0_conv_ln0_g": _L0_conv_in["ln0_g"],
        "L0_conv_ln0_b": _L0_conv_in["ln0_b"],
        "L0_conv_ln1_g": _L0_conv_in["ln1_g"],
        "L0_conv_ln1_b": _L0_conv_in["ln1_b"],
        "L0_conv_ln2_g": _L0_conv_in["ln2_g"],
        "L0_conv_ln2_b": _L0_conv_in["ln2_b"],
        "L0_conv_W_out": _L0_conv_in["W_out"],
        "L0_conv_W_whiten": _L0_conv_in["W_whiten"],
        "L0_conv_W_key": _L0_conv_in["W_key"],
        "L0_conv_W_recep": _L0_conv_in["W_recep"],
        "L0_conv_W_value": _L0_conv_in["W_value"],
        "L1_conv_Wq": _L1_conv_in["Wq"],
        "L1_conv_Wk": _L1_conv_in["Wk"],
        "L1_conv_Wv": _L1_conv_in["Wv"],
        "L1_conv_B": _L1_conv_in["B"],
        "L1_conv_Wm": _L1_conv_in["Wm"],
    }

def reference(x, L0_conv_ln0_g, L0_conv_ln0_b, L0_conv_ln1_g, L0_conv_ln1_b, L0_conv_ln2_g, L0_conv_ln2_b, L0_conv_W_out, L0_conv_W_whiten, L0_conv_W_key, L0_conv_W_recep, L0_conv_W_value, L1_conv_Wq, L1_conv_Wk, L1_conv_Wv, L1_conv_B, L1_conv_Wm):
    import jax
    import jax.numpy as jnp
    def _L0_conv_ref(inp_img, ln0_g, ln0_b, ln1_g, ln1_b, ln2_g, ln2_b, W_out, W_whiten, W_key, W_recep, W_value):
        import jax, jax.numpy as jnp
        import numpy as np
        DIM = 128
        HID = 4 * DIM
        EPS = 1e-05

        def _ln(x, g, b):
            mu = jnp.mean(x, axis=-1, keepdims=True)
            var = jnp.mean(jnp.square(x - mu), axis=-1, keepdims=True)
            return (x - mu) * jax.lax.rsqrt(var + EPS) * g + b

        def _block(x, ln0_g, ln0_b, ln1_g, ln1_b, ln2_g, ln2_b, W_out, W_whiten, W_key, W_recep, W_value):
            b, c, h, w = x.shape
            t = x.reshape(b, c, h * w).transpose(0, 2, 1)
            t = _ln(t, ln0_g, ln0_b)
            y1 = _ln(t, ln1_g, ln1_b)
            att = jnp.einsum('btc,oc->bto', jax.nn.sigmoid(y1) * y1, W_out)
            t = t + att
            y2 = _ln(t, ln2_g, ln2_b)
            wht = jnp.einsum('btc,oc->bto', y2, W_whiten)
            k = jnp.square(jax.nn.relu(jnp.einsum('btc,hc->bth', wht, W_key)))
            kv = jnp.einsum('bth,ch->btc', k, W_value)
            r = jax.nn.sigmoid(jnp.einsum('btc,oc->bto', wht, W_recep))
            t = t + r * kv
            return t.transpose(0, 2, 1).reshape(b, c, h, w)
        params = (ln0_g, ln0_b, ln1_g, ln1_b, ln2_g, ln2_b, W_out, W_whiten, W_key, W_recep, W_value)
        out1 = _block(inp_img, *params)
        out2 = _block(inp_img.transpose(0, 1, 3, 2), *params).transpose(0, 1, 3, 2)
        return out2 + out1

    def _L1_conv_ref(x, Wq, Wk, Wv, B, Wm):
        import jax, jax.numpy as jnp
        import numpy as np
        BS, C, H, W = (4, 128, 64, 64)
        IC = C // 2
        bs, c, h, w = x.shape
        xf = x.reshape(bs, c, h * w)
        q = jnp.einsum('jc,bct->bjt', Wq, xf)
        k = jnp.einsum('jc,bct->bjt', Wk, xf)
        v = jnp.einsum('jc,bct->bjt', Wv, xf)
        ek = jnp.exp(k)
        eB = jnp.exp(B)
        num = jnp.einsum('ji,bit->bjt', eB, ek * v)
        den = jnp.einsum('ji,bit->bjt', eB, ek)
        out = q * (num / den)
        out = jnp.einsum('oj,bjt->bot', Wm, out)
        return out.reshape(bs, c, h, w)

    def _gn(v, G=32, eps=1e-5):
        B_, C_, H_, W_ = v.shape
        g = v.reshape(B_, G, C_ // G, H_, W_)
        m = jnp.mean(g, axis=(2, 3, 4), keepdims=True)
        s = jnp.var(g, axis=(2, 3, 4), keepdims=True)
        return ((g - m) / jnp.sqrt(s + eps)).reshape(v.shape)

    def _ln_c(v, eps=1e-6):
        m = jnp.mean(v, axis=1, keepdims=True)
        s = jnp.var(v, axis=1, keepdims=True)
        return (v - m) / jnp.sqrt(s + eps)

    def _ln_t(v, eps=1e-5):
        m = jnp.mean(v, axis=-1, keepdims=True)
        s = jnp.var(v, axis=-1, keepdims=True)
        return (v - m) / jnp.sqrt(s + eps)

    def _to_tokens(v):
        B_, C_, H_, W_ = v.shape
        return v.reshape(B_, C_, H_ * W_).transpose(0, 2, 1)
    def _from_tokens(t, like):
        B_, C_, H_, W_ = like.shape
        return t.transpose(0, 2, 1).reshape(B_, C_, H_, W_)

    x = x + _L0_conv_ref(_gn(x), L0_conv_ln0_g, L0_conv_ln0_b, L0_conv_ln1_g, L0_conv_ln1_b, L0_conv_ln2_g, L0_conv_ln2_b, L0_conv_W_out, L0_conv_W_whiten, L0_conv_W_key, L0_conv_W_recep, L0_conv_W_value)
    x = x + _L1_conv_ref(_gn(x), L1_conv_Wq, L1_conv_Wk, L1_conv_Wv, L1_conv_B, L1_conv_Wm)
    return x


_drawn_inputs = setup_inputs


def setup_inputs(seed=0):
    import zlib

    import numpy as np

    out = dict(_drawn_inputs(seed))
    spreads = {'L0_conv_ln0_g': (1.0, 0.2),
     'L0_conv_ln0_b': (0.0, 0.1),
     'L0_conv_ln1_g': (1.0, 0.2),
     'L0_conv_ln1_b': (0.0, 0.401),
     'L0_conv_ln2_g': (1.0, 0.6),
     'L0_conv_ln2_b': (0.0, 0.8)}
    factors = {'L0_conv_W_recep': 6.868, 'L1_conv_B': 47.007}
    for name, (base, spread) in spreads.items():
        noise = np.random.default_rng([zlib.crc32(name.encode()), seed]).standard_normal(out[name].shape)
        drawn = base * np.exp(spread * noise) if base else spread * noise
        out[name] = jnp.asarray(drawn.astype(out[name].dtype))
    for name, factor in factors.items():
        out[name] = (out[name] * factor).astype(out[name].dtype)
    return out
```

```python
from contextlib import ExitStack

import numpy as np

import concourse.bass as bass
from concourse import mybir

F32 = mybir.dt.float32
ALU = mybir.AluOpType
ACT = mybir.ActivationFunctionType

C = 128
IMAGES = 4
PIXELS = 128 * 128
TILE = 512
TILES = PIXELS // TILE
CHUNKS = TILE // 128
HID = 512
HJ = HID // 128
IC = C // 2
PAIRS = TILES // 2
GROUP = C // 32
EPS = 1e-5
LAG = 3
LAG_B = 2
FIRST_LOADS = 8
STORES = 8


def preact_kernel(nc, x, consts, vecs, w_whiten, w_key_t, w_recep_t, w_value_t, w_out_t,
                  w_qkv_t, b_t, w_m_t, out):
    with ExitStack() as ctx:
        def sb(name, cols):
            return ctx.enter_context(nc.sbuf_tensor(name, [C, cols], F32))

        def sem(name):
            return ctx.enter_context(nc.semaphore(name))

        xs = sb("xs", 2 * PIXELS)

        cst = sb("cst", 3 * C)
        centre, group_mean, ident = (cst[:, i * C:(i + 1) * C] for i in range(3))
        vec = sb("vec", 6)
        g0, b0, g1, b1, g2, b2 = (vec[:, i:i + 1] for i in range(6))
        mean_col = sb("mean_col", 1)
        whiten = sb("whiten", C)
        key_t = sb("key_t", HID)
        recep_t = sb("recep_t", C)
        value_t = sb("value_t", HJ * C)
        out_t = sb("out_t", C)
        qkv_t = sb("qkv_t", 3 * IC)
        bt = sb("bt", IC)
        wm_t = sb("wm_t", C)

        raw_kr = sb("raw_kr", HID + C)
        scl_kr = sb("scl_kr", HID + C)
        wkr = sb("wkr", HID + C)
        bias_kr = sb("bias_kr", HJ + 1)
        half_bias_r = sb("half_bias_r", 1)
        w_c0 = sb("w_c0", C)
        w_c1 = sb("w_c1", C)
        bias_c0 = sb("bias_c0", 1)
        bias_c1 = sb("bias_c1", 1)
        exp_b = sb("exp_b", C)

        gn_in = sb("gn_in", TILES * 6)
        gn_out = sb("gn_out", TILES * 6)
        gn_mv = sb("gn_mv", 2)
        gn_tmp = sb("gn_tmp", 4)
        gn_gain = sb("gn_gain", 1)
        gn_shift = sb("gn_shift", 1)
        minus_half = sb("minus_half", CHUNKS)

        cs0, cs1, sq0, sq1, z0, z1, s, t0, t1, z2, th, ff = (
            sb(n, TILE) for n in ("cs0", "cs1", "sq0", "sq1", "z0", "z1", "s", "t0", "t1", "z2", "th", "ff"))
        kk = sb("kk", HJ * TILE)
        var0, var1, var2 = (sb(n, CHUNKS) for n in ("var0", "var1", "var2"))
        r0, r1, r2 = (sb(n, CHUNKS) for n in ("r0", "r1", "r2"))
        bs2 = sb("bs2", CHUNKS * 6)
        apart, within, between = (sb(n, CHUNKS) for n in ("apart", "within", "between"))
        scratch = sb("scratch", 1)

        e, vs, ev, rec, ratio, o, os0, os1 = cs0, cs1, sq0, sq1, z0, z1, s, t0
        qs, gx0, gx1 = t1, z2, th

        bank = [ctx.enter_context(nc.psum_tensor(f"bank{i}", [C, TILE], F32)) for i in range(8)]
        small = bank[7]

        first_loaded = [sem(f"first_loaded{i}") for i in range(FIRST_LOADS)]
        weights_loaded = sem("weights_loaded")
        x_loaded = sem("x_loaded")
        stored = sem("stored")
        consts_set = sem("consts_set")
        setup_pe = sem("setup_pe")
        setup_dve = sem("setup_dve")
        exp_b_ready = sem("exp_b_ready")
        gn_pe = sem("gn_pe")
        gn_dve = sem("gn_dve")
        gn_pow = sem("gn_pow")
        in_stats = sem("in_stats")

        c0_done, c1_done, w_done, k_done, r_done, v_done = map(
            sem, ("c0_done", "c1_done", "w_done", "k_done", "r_done", "v_done"))
        st0_done, st1_done, tr2_done, bc0_done, bc1_done, bc2_done = map(
            sem, ("st0_done", "st1_done", "tr2_done", "bc0_done", "bc1_done", "bc2_done"))
        cs0_ready, cs1_ready, sq1_ready, relu_ready, tanh_ready, silu_ready, t0_ready = map(
            sem, ("cs0_ready", "cs1_ready", "sq1_ready", "relu_ready", "tanh_ready", "silu_ready", "t0_ready"))
        sq0_ready, k_ready, r0_ready, r1_ready, r2_ready = map(
            sem, ("sq0_ready", "k_ready", "r0_ready", "r1_ready", "r2_ready"))
        t1_ready, acc_ready, var0_ready, var1_ready, var2_ready = map(
            sem, ("t1_ready", "acc_ready", "var0_ready", "var1_ready", "var2_ready"))
        bs2_ready, mv2_ready, z0_ready, z1_ready, z2_ready, ff_ready, x1_ready, x1_stats = map(
            sem, ("bs2_ready", "mv2_ready", "z0_ready", "z1_ready", "z2_ready", "ff_ready", "x1_ready", "x1_stats"))
        kb_done, vb_done, den_done, num_done, qb_done, ob_done = map(
            sem, ("kb_done", "vb_done", "den_done", "num_done", "qb_done", "ob_done"))
        gx_ready, e_ready, vs_ready, qs_ready, os_ready = map(
            sem, ("gx_ready", "e_ready", "vs_ready", "qs_ready", "os_ready"))
        ev_ready, rec_ready, ratio_ready, o_ready, y_ready = map(
            sem, ("ev_ready", "rec_ready", "ratio_ready", "o_ready", "y_ready"))

        GN_DVE_A, GN_PE_A = 0, 0
        GN_DVE_B, GN_PE_B = 8, 3
        GN_DVE_IMAGE, GN_PE_IMAGE = 14, 5
        SETUP_BANKS = 3

        def tile_at(b, t):
            return xs[:, bass.ds((b % 2) * PIXELS + t * TILE, TILE)]

        def images(eng):
            with eng.Fori(0, IMAGES - 1) as b:
                yield b, False
            yield IMAGES - 1, True

        def steps(eng, count, lag, drain=None):
            yield from range(lag + 1)
            with eng.Fori(lag + 1, count) as t:
                yield t
            yield from range(count, count + (drain or lag))

        def on(t, lag, count):
            return not isinstance(t, int) or lag <= t < count + lag

        def wait(eng, sem_, b, local, per_image, each=1):
            if isinstance(local, int) and local <= 0:
                return
            eng.wait_ge(sem_, (b * per_image + local) * each)

        block = ctx.enter_context(nc.Block())

        @block.sync
        def _(sp):
            cols = PIXELS // FIRST_LOADS
            for dst, src in ((cst, consts), (vec, vecs)):
                sp.dma_start(dst[:, :], src).then_inc(weights_loaded, 16)
            for i in range(FIRST_LOADS):
                sp.dma_start(xs[:, i * cols:(i + 1) * cols], x[0, :, i * cols:(i + 1) * cols])\
                  .then_inc(first_loaded[i], 16)
            for dst, src in ((whiten, w_whiten), (key_t, w_key_t), (recep_t, w_recep_t), (out_t, w_out_t),
                             (qkv_t, w_qkv_t), (bt, b_t), (wm_t, w_m_t)):
                sp.dma_start(dst[:, :], src).then_inc(weights_loaded, 16)
            sp.dma_start(value_t[:, :].rearrange("p (j c) -> p j c", j=HJ),
                         w_value_t.rearrange("(j p) c -> p j c", p=C)).then_inc(weights_loaded, 16)

            def load_image(b):
                def load(t):
                    sp.dma_start(tile_at(b, t), x[b, :, bass.ts(t, TILE)]).then_inc(x_loaded, 16)

                if not isinstance(b, int):
                    sp.wait_ge(stored, (b - 1) * STORES * 16)
                load(0)
                with sp.Fori(1, TILES) as t:
                    sp.wait_ge(x_loaded, ((b - 1) * TILES + t) * 16)
                    load(t)

            def store_image(b):
                n = PIXELS // STORES
                with sp.Fori(0, STORES) as i:
                    sp.wait_ge(y_ready, b * TILES + (i + 1) * (TILES // STORES))
                    sp.dma_start(out[b, :, bass.ts(i, n)], xs[:, bass.ds((b % 2) * PIXELS + i * n, n)])\
                      .then_inc(stored, 16)

            load_image(1)
            with sp.Fori(0, IMAGES - 2) as b:
                store_image(b)
                load_image(b + 2)
            with sp.Fori(IMAGES - 2, IMAGES) as b:
                store_image(b)
            sp.wait_ge(stored, IMAGES * STORES * 16)

        @block.tensor
        def _(pe):
            mm = nc.tensor.matmul

            def one(dst, lhs, rhs):
                return mm(dst, lhs, rhs, start=True, stop=True)

            pe.wait_ge(weights_loaded, 10 * 16)
            one(bank[0][:, :], whiten[:, :], key_t[:, :])
            one(bank[1][:, 0:C], whiten[:, :], recep_t[:, :]).then_inc(setup_pe, 1)
            pe.wait_ge(setup_dve, 2)
            for j in range(HJ + 1):
                one(bank[2][:, j:j + 1], raw_kr[:, j * C:(j + 1) * C], b2)
            one(bank[2][:, HJ + 1:HJ + 2], centre, b0).then_inc(setup_pe, 1)
            pe.wait_ge(setup_dve, 3)
            one(bank[0][:, :], centre, scl_kr[:, 0:HID])
            one(bank[1][:, 0:C], centre, scl_kr[:, HID:HID + C]).then_inc(setup_pe, 1)

            def group_norm(b, base_dve):
                pe.wait_ge(gn_dve, b * GN_DVE_IMAGE + base_dve + 1)
                one(small[:, 0:1], group_mean, gn_mv[:, 0:1]).then_inc(gn_pe, 1)
                pe.wait_ge(gn_dve, b * GN_DVE_IMAGE + base_dve + 4)
                one(small[:, 1:2], group_mean, gn_tmp[:, 2:3]).then_inc(gn_pe, 1)

            for b, last_image in images(pe):
                group_norm(b, GN_DVE_A)
                pe.wait_ge(gn_dve, b * GN_DVE_IMAGE + GN_DVE_A + 6)
                one(small[:, 2:3], centre, gn_shift[:, :]).then_inc(gn_pe, 1)
                pe.wait_ge(gn_dve, b * GN_DVE_IMAGE + GN_DVE_A + 8)
                for t in steps(pe, TILES, LAG):
                    def need(sem_, local, each=1):
                        wait(pe, sem_, b, local, TILES, each)

                    def keys(j):
                        if on(t, 3, TILES):
                            if j == 0:
                                need(z2_ready, t - 2)
                            wait(pe, relu_ready, b, (t - 3) * HJ + j - 1, TILES * HJ)
                            one(bank[2 + j % 2][:, :], wkr[:, j * C:(j + 1) * C], z2[:, :]).then_inc(k_done, 1)

                    def values(j):
                        if on(t, 3, TILES):
                            if j == 0:
                                need(ff_ready, t - 3)
                            wait(pe, k_ready, b, (t - 3) * HJ + j + 1, TILES * HJ)
                            i = mm(bank[4][:, :], value_t[:, j * C:(j + 1) * C], kk[:, j * TILE:(j + 1) * TILE],
                                   start=(j == 0), stop=(j == HJ - 1))
                            if j == HJ - 1:
                                i.then_inc(v_done, 1)

                    def column_sums(squares, at):
                        for j in range(CHUNKS):
                            last = one(small[:, at + j:at + j + 1], squares[:, j * 128:(j + 1) * 128], mean_col[:, :])
                        return last

                    def spread(dst, r):
                        for j in range(CHUNKS):
                            last = nc.tensor.transpose(dst[:, j * 128:(j + 1) * 128],
                                                       r[:, j:j + 1].to_broadcast([C, C]), ident)
                        return last

                    if on(t, 0, TILES):
                        need(t1_ready, t - 2)
                        one(bank[0][:, :], w_c0[:, :], tile_at(b, t)).then_inc(c0_done, 1)
                    if on(t, 1, TILES):
                        need(z0_ready, t)
                        need(bs2_ready, t - 2)
                        one(bank[1][:, :], w_c1[:, :], z0[:, :]).then_inc(c1_done, 1)
                    keys(0)
                    if on(t, 2, TILES):
                        need(silu_ready, t - 1)
                        need(cs0_ready, t + 1 if on(t, 0, TILES) else TILES)
                        one(bank[0][:, :], out_t[:, :], s[:, :]).then_inc(w_done, 1)
                    keys(1)
                    if on(t, 0, TILES):
                        need(sq0_ready, t + 1)
                        need(var1_ready, t - 1)
                        column_sums(sq0, 0).then_inc(st0_done, 1)
                    keys(2)
                    if on(t, 2, TILES):
                        need(t1_ready, t - 1)
                        need(sq1_ready, t if on(t, 1, TILES) else TILES)
                        for j in range(CHUNKS):
                            last = nc.tensor.transpose(bank[1][:, j * 128:(j + 1) * 128],
                                                       t1[:, j * 128:(j + 1) * 128], ident)
                        last.then_inc(tr2_done, 1)
                    keys(3)
                    if on(t, 1, TILES):
                        need(sq1_ready, t)
                        need(var0_ready, t + 1 if on(t, 0, TILES) else TILES)
                        column_sums(sq1, CHUNKS).then_inc(st1_done, 1)
                    if on(t, 3, TILES):
                        need(z1_ready, t - 1 if on(t, 2, TILES) else TILES)
                        one(bank[6][:, :], wkr[:, HID:HID + C], z2[:, :]).then_inc(r_done, 1)
                    if on(t, 0, TILES):
                        need(r0_ready, t + 1)
                        need(z2_ready, t - 2)
                        spread(bank[5], r0).then_inc(bc0_done, 1)
                    values(0)
                    values(1)
                    if on(t, 1, TILES):
                        need(r1_ready, t)
                        need(tanh_ready, t - 2)
                        need(z1_ready, t - 1)
                        spread(bank[6], r1).then_inc(bc1_done, 1)
                    values(2)
                    if on(t, 2, TILES):
                        need(r2_ready, t - 1)
                        need(z0_ready, t + 1 if on(t, 0, TILES) else TILES)
                        spread(bank[5], r2).then_inc(bc2_done, 1)
                    values(3)

                group_norm(b, GN_DVE_B)
                for p in steps(pe, PAIRS, LAG_B):
                    def need(sem_, local, each=1):
                        wait(pe, sem_, b, local, PAIRS, each)

                    def project(dst, which):
                        w = qkv_t[:, which * IC:(which + 1) * IC]
                        one(dst[0:IC, :], w, gx0[:, :])
                        return one(dst[IC:C, :], w, gx1[:, :])

                    if on(p, 0, PAIRS):
                        need(gx_ready, p + 1, 2)
                        need(e_ready, p)
                        project(bank[0], 1).then_inc(kb_done, 1)
                        need(vs_ready, p)
                        project(bank[1], 2).then_inc(vb_done, 1)
                        need(qs_ready, p)
                        project(bank[4], 0).then_inc(qb_done, 1)
                    if on(p, 1, PAIRS):
                        need(e_ready, p)
                        need(rec_ready, p - 1)
                        one(bank[2][:, :], exp_b[:, :], e[:, :]).then_inc(den_done, 1)
                        need(ev_ready, p)
                        need(ratio_ready, p - 1)
                        one(bank[3][:, :], exp_b[:, :], ev[:, :]).then_inc(num_done, 1)
                    if on(p, 2, PAIRS):
                        need(o_ready, p - 1)
                        need(os_ready, p - 2, 2)
                        one(bank[5][:, :], wm_t[0:IC, :], o[0:IC, :])
                        one(bank[6][:, :], wm_t[IC:C, :], o[IC:C, :]).then_inc(ob_done, 1)

        @block.scalar
        def _(act):
            f = nc.scalar.activation
            act.wait_ge(consts_set, 2)
            act.wait_ge(weights_loaded, 10 * 16)
            for h in range(2):
                q = slice(h * IC, (h + 1) * IC)
                last = f(exp_b[q, q], bt[q, :], ACT.Exp)
            last.then_inc(exp_b_ready, 1)

            for b, last_image in images(act):
                for t in steps(act, TILES, LAG):
                    def need(sem_, local, each=1):
                        wait(act, sem_, b, local, TILES, each)

                    def relu(j):
                        if on(t, 3, TILES):
                            if j == 0:
                                need(v_done, t - 3)
                            wait(act, k_done, b, (t - 3) * HJ + j + 1, TILES * HJ)
                            f(kk[:, j * TILE:(j + 1) * TILE], bank[2 + j % 2][:, :], ACT.Relu,
                              bias=bias_kr[:, j:j + 1]).then_inc(relu_ready, 1)

                    if on(t, 0, TILES):
                        need(c0_done, t + 1)
                        need(z0_ready, t)
                        f(cs0[:, :], bank[0][:, :], ACT.Identity, bias=bias_c0[:, :]).then_inc(cs0_ready, 1)
                    if on(t, 1, TILES):
                        need(c1_done, t)
                        need(z1_ready, t - 1)
                        f(cs1[:, :], bank[1][:, :], ACT.Identity, bias=bias_c1[:, :]).then_inc(cs1_ready, 1)
                        need(st1_done, t - 1)
                        f(sq1[:, :], bank[1][:, :], ACT.Square, bias=bias_c1[:, :]).then_inc(sq1_ready, 1)
                    relu(0)
                    relu(1)
                    if on(t, 1, TILES):
                        need(z0_ready, t)
                        need(t1_ready, t - 1)
                        f(t0[:, :], z0[:, :], ACT.Identity, bias=b0, scale=g0).then_inc(t0_ready, 1)
                    relu(2)
                    relu(3)
                    if on(t, 3, TILES):
                        need(r_done, t - 2)
                        need(ff_ready, t - 3)
                        f(th[:, :], bank[6][:, :], ACT.Tanh, bias=half_bias_r[:, :], scale=0.5)\
                            .then_inc(tanh_ready, 1)
                    if on(t, 1, TILES):
                        need(z1_ready, t)
                        need(w_done, t - 1)
                        f(s[:, :], z1[:, :], ACT.Silu, bias=b1, scale=g1).then_inc(silu_ready, 1)

                act.wait_ge(gn_dve, (b + 1) * GN_DVE_IMAGE)
                for p in steps(act, PAIRS, LAG_B):
                    def need(sem_, local, each=1):
                        wait(act, sem_, b, local, PAIRS, each)

                    if on(p, 0, PAIRS):
                        need(qb_done, p)
                        for h, g in enumerate((gx0, gx1)):
                            f(g[:, :], tile_at(b, p * 2 + h), ACT.Identity, bias=gn_shift[:, :],
                              scale=gn_gain[:, :]).then_inc(gx_ready, 1)
                    if on(p, 1, PAIRS):
                        need(qb_done, p)
                        need(o_ready, p - 1)
                        f(qs[:, :], bank[4][:, :], ACT.Copy).then_inc(qs_ready, 1)
                    if on(p, 0, PAIRS):
                        need(kb_done, p + 1)
                        need(den_done, p)
                        need(ev_ready, p)
                        f(e[:, :], bank[0][:, :], ACT.Exp).then_inc(e_ready, 1)
                        need(vb_done, p + 1)
                        f(vs[:, :], bank[1][:, :], ACT.Copy).then_inc(vs_ready, 1)
                    if on(p, 2, PAIRS):
                        need(ob_done, p - 1)
                        need(y_ready, p - 2, 2)
                        f(os0[:, :], bank[5][:, :], ACT.Copy).then_inc(os_ready, 1)
                        f(os1[:, :], bank[6][:, :], ACT.Copy).then_inc(os_ready, 1)

        @block.gpsimd
        def _(pool):
            tt = nc.gpsimd.tensor_tensor
            nc.gpsimd.memset(minus_half[:, :], -0.5).then_inc(consts_set, 1)
            nc.gpsimd.memset(exp_b[:, :], 0.0).then_inc(consts_set, 1)
            pool.wait_ge(consts_set, 2)

            def group_norm(b, base_dve, n):
                pool.wait_ge(gn_dve, b * GN_DVE_IMAGE + base_dve + 5)
                tt(gn_gain[:, :], gn_tmp[:, 3:4], minus_half[:, 0:1], ALU.pow).then_inc(gn_pow, 1)

            for b, last_image in images(pool):
                group_norm(b, GN_DVE_A, 1)
                for t in steps(pool, TILES, LAG):
                    def need(sem_, local, each=1):
                        wait(pool, sem_, b, local, TILES, each)

                    def square(j):
                        if on(t, 3, TILES):
                            wait(pool, relu_ready, b, (t - 3) * HJ + j + 1, TILES * HJ)
                            k = kk[:, j * TILE:(j + 1) * TILE]
                            tt(k, k, k, ALU.mult).then_inc(k_ready, 1)

                    def rsqrt(r, var):
                        return tt(r[:, :], var[:, :], minus_half[:, :], ALU.pow)

                    if on(t, 0, TILES):
                        need(cs0_ready, t + 1)
                        need(st0_done, t)
                        tt(sq0[:, :], cs0[:, :], cs0[:, :], ALU.mult).then_inc(sq0_ready, 1)
                    square(0)
                    square(1)
                    if on(t, 0, TILES):
                        need(var0_ready, t + 1)
                        need(bc0_done, t)
                        rsqrt(r0, var0).then_inc(r0_ready, 1)
                    square(2)
                    if on(t, 2, TILES):
                        need(var2_ready, t - 1)
                        need(bc2_done, t - 2)
                        rsqrt(r2, var2).then_inc(r2_ready, 1)
                    if on(t, 1, TILES):
                        need(var1_ready, t)
                        need(bc1_done, t - 1)
                        rsqrt(r1, var1).then_inc(r1_ready, 1)
                    square(3)

                group_norm(b, GN_DVE_B, 2)
                for p in steps(pool, PAIRS, LAG_B):
                    def need(sem_, local, each=1):
                        wait(pool, sem_, b, local, PAIRS, each)

                    if on(p, 0, PAIRS):
                        need(vs_ready, p + 1)
                        need(e_ready, p + 1)
                        need(num_done, p)
                        tt(ev[:, :], e[:, :], vs[:, :], ALU.mult).then_inc(ev_ready, 1)
                    if on(p, 2, PAIRS):
                        for h, part in enumerate((os0, os1)):
                            wait(pool, os_ready, b, (p - 2) * 2 + h + 1, PAIRS * 2)
                            y = tile_at(b, (p - 2) * 2 + h)
                            tt(y, y, part[:, :], ALU.add).then_inc(y_ready, 1)

        @block.vector
        def _(dve):
            v = nc.vector
            v.memset(mean_col[:, :], 1.0 / C)
            for t in range(TILES):
                if t % (TILES // FIRST_LOADS) == 0:
                    dve.wait_ge(first_loaded[t // (TILES // FIRST_LOADS)], 16)
                v.bn_stats(gn_in[:, t * 6:(t + 1) * 6], xs[:, t * TILE:(t + 1) * TILE]).then_inc(in_stats, 1)

            dve.wait_ge(setup_pe, 1)
            v.tensor_copy(raw_kr[:, 0:HID], bank[0][:, :]).then_inc(setup_dve, 1)
            v.tensor_copy(raw_kr[:, HID:HID + C], bank[1][:, 0:C]).then_inc(setup_dve, 1)
            dve.wait_ge(setup_dve, 2)
            v.tensor_scalar(scl_kr[:, :], raw_kr[:, :], g2, None, ALU.mult).then_inc(setup_dve, 1)
            dve.wait_ge(setup_pe, 2)
            v.tensor_copy(bias_kr[:, :], bank[2][:, 0:HJ + 1]).then_inc(setup_dve, 1)
            v.tensor_copy(bias_c1[:, :], bank[2][:, HJ + 1:HJ + 2]).then_inc(setup_dve, 1)
            v.tensor_scalar(half_bias_r[:, :], bank[2][:, HJ:HJ + 1], 0.5, None, ALU.mult).then_inc(setup_dve, 1)
            v.tensor_scalar(w_c1[:, :], centre, g0, None, ALU.mult).then_inc(setup_dve, 1)
            dve.wait_ge(setup_pe, 3)
            v.tensor_copy(wkr[:, 0:HID], bank[0][:, :]).then_inc(setup_dve, 1)
            v.tensor_copy(wkr[:, HID:HID + C], bank[1][:, 0:C]).then_inc(setup_dve, 1)
            dve.wait_ge(setup_dve, 9)
            dve.wait_ge(exp_b_ready, 1)

            def group_norm(b, stats, base_dve, base_pe, n_pow):
                def at(n):
                    return b * GN_DVE_IMAGE + base_dve + n

                def pe_at(n):
                    return b * GN_PE_IMAGE + base_pe + n

                mean, var = gn_mv[:, 0:1], gn_mv[:, 1:2]
                off, off2, about, group_var = (gn_tmp[:, i:i + 1] for i in range(4))
                v.memset(scratch[:, :], 0.0)
                v.bn_aggr(gn_mv[:, :], stats[:, :]).then_inc(gn_dve, 1)
                dve.wait_ge(gn_pe, pe_at(1))
                v.tensor_tensor(off, mean, small[:, 0:1], ALU.subtract).then_inc(gn_dve, 1)
                dve.wait_ge(gn_dve, at(2))
                v.tensor_tensor(off2, off, off, ALU.mult).then_inc(gn_dve, 1)
                dve.wait_ge(gn_dve, at(3))
                v.tensor_tensor(about, var, off2, ALU.add).then_inc(gn_dve, 1)
                dve.wait_ge(gn_pe, pe_at(2))
                v.tensor_scalar(group_var, small[:, 1:2], EPS, None, ALU.add).then_inc(gn_dve, 1)
                dve.wait_ge(gn_pow, b * 2 + n_pow)
                v.scalar_tensor_tensor(out=gn_shift[:, :], in0=small[:, 0:1], scalar=-1.0,
                                       in1=gn_gain[:, :], op0=ALU.mult, op1=ALU.mult).then_inc(gn_dve, 1)

            for b, last_image in images(dve):
                dve.wait_ge(in_stats, (b + 1) * TILES)
                group_norm(b, gn_in, GN_DVE_A, GN_PE_A, 1)
                v.tensor_scalar(w_c0[:, :], centre, gn_gain[:, :], None, ALU.mult).then_inc(gn_dve, 1)
                dve.wait_ge(gn_pe, b * GN_PE_IMAGE + 3)
                v.tensor_copy(bias_c0[:, :], small[:, 2:3]).then_inc(gn_dve, 1)

                for t in steps(dve, TILES, LAG, LAG + 1):
                    def need(sem_, local, each=1):
                        wait(dve, sem_, b, local, TILES, each)

                    if on(t, 2, TILES):
                        need(w_done, t - 1)
                        need(t0_ready, t - 1)
                        need(tr2_done, t - 2)
                        need(acc_ready, t - 2)
                        v.tensor_tensor(t1[:, :], bank[0][:, :], t0[:, :], ALU.add).then_inc(t1_ready, 1)
                        need(t1_ready, t - 1)
                        acc = tile_at(b, t - 2)
                        v.scalar_tensor_tensor(out=acc, in0=t1[:, :], scalar=2.0, in1=acc,
                                               op0=ALU.mult, op1=ALU.add).then_inc(acc_ready, 1)
                    if on(t, 0, TILES):
                        need(st0_done, t + 1)
                        need(r0_ready, t)
                        v.tensor_scalar(var0[:, :], small[:, 0:CHUNKS], EPS, None, ALU.add).then_inc(var0_ready, 1)
                    if on(t, 2, TILES):
                        need(tr2_done, t - 1)
                        for j in range(CHUNKS):
                            v.bn_stats(bs2[:, j * 6:(j + 1) * 6], bank[1][:, j * 128:(j + 1) * 128])\
                             .then_inc(bs2_ready, 1)
                        need(bs2_ready, t - 1, CHUNKS)
                        v.tensor_tensor(apart[:, :], bs2[:, 1::6], bs2[:, 4::6], ALU.subtract).then_inc(mv2_ready, 1)
                        v.scalar_tensor_tensor(out=within[:, :], in0=bs2[:, 2::6], scalar=C * EPS, in1=bs2[:, 5::6],
                                               op0=ALU.add, op1=ALU.add).then_inc(mv2_ready, 1)
                        wait(dve, mv2_ready, b, (t - 2) * 3 + 1, TILES * 3)
                        v.scalar_tensor_tensor(out=between[:, :], in0=apart[:, :], scalar=0.25, in1=apart[:, :],
                                               op0=ALU.mult, op1=ALU.mult).then_inc(mv2_ready, 1)
                        need(mv2_ready, t - 1, 3)
                        need(r2_ready, t - 2)
                        v.scalar_tensor_tensor(out=var2[:, :], in0=within[:, :], scalar=1.0 / C, in1=between[:, :],
                                               op0=ALU.mult, op1=ALU.add).then_inc(var2_ready, 1)
                    if on(t, 1, TILES):
                        need(st1_done, t)
                        need(r1_ready, t - 1)
                        v.tensor_scalar(var1[:, :], small[:, CHUNKS:2 * CHUNKS], EPS, None, ALU.add)\
                         .then_inc(var1_ready, 1)
                    if on(t, 0, TILES):
                        if not last_image:
                            dve.wait_ge(x_loaded, (b * TILES + t + 1) * 16)
                        need(bc0_done, t + 1)
                        need(c1_done, t)
                        need(t0_ready, t)
                        v.tensor_tensor(z0[:, :], cs0[:, :], bank[5][:, :], ALU.mult).then_inc(z0_ready, 1)
                        if not last_image:
                            v.bn_stats(gn_in[:, bass.ds(t * 6, 6)], tile_at(b + 1, t)).then_inc(in_stats, 1)
                    if on(t, 1, TILES):
                        need(bc1_done, t)
                        need(silu_ready, t - 1)
                        v.tensor_tensor(z1[:, :], cs1[:, :], bank[6][:, :], ALU.mult).then_inc(z1_ready, 1)
                    if on(t, 2, TILES):
                        need(bc2_done, t - 1)
                        need(r_done, t - 2)
                        v.tensor_tensor(z2[:, :], t1[:, :], bank[5][:, :], ALU.mult).then_inc(z2_ready, 1)
                    if on(t, 4, TILES):
                        need(x1_ready, t - 3)
                    if on(t, 3, TILES):
                        need(v_done, t - 2)
                        need(tanh_ready, t - 2)
                        v.scalar_tensor_tensor(out=ff[:, :], in0=th[:, :], scalar=1.0, in1=bank[4][:, :],
                                               op0=ALU.add, op1=ALU.mult).then_inc(ff_ready, 1)
                    elif on(t, 4, TILES):
                        v.memset(scratch[:, :], 0.0)
                    if on(t, 4, TILES):
                        v.bn_stats(gn_out[:, bass.ds((t - 4) * 6, 6)], tile_at(b, t - 4)).then_inc(x1_stats, 1)
                    if on(t, 3, TILES):
                        need(ff_ready, t - 2)
                        x1 = tile_at(b, t - 3)
                        v.tensor_tensor(x1, x1, ff[:, :], ALU.add).then_inc(x1_ready, 1)

                dve.wait_ge(x1_stats, (b + 1) * TILES)
                group_norm(b, gn_out, GN_DVE_B, GN_PE_B, 2)

                for p in steps(dve, PAIRS, LAG_B):
                    def need(sem_, local, each=1):
                        wait(dve, sem_, b, local, PAIRS, each)

                    if on(p, 1, PAIRS):
                        need(den_done, p)
                        need(ratio_ready, p - 1)
                        v.reciprocal(rec[:, :], bank[2][:, :]).then_inc(rec_ready, 1)
                        need(num_done, p)
                        need(rec_ready, p)
                        v.tensor_tensor(ratio[:, :], rec[:, :], bank[3][:, :], ALU.mult).then_inc(ratio_ready, 1)
                        need(qs_ready, p)
                        need(ratio_ready, p)
                        need(ob_done, p - 1)
                        v.tensor_tensor(o[:, :], qs[:, :], ratio[:, :], ALU.mult).then_inc(o_ready, 1)
                dve.wait_ge(y_ready, (b + 1) * TILES)


def kernel(**inputs):
    import concourse.bacc as bacc
    from concourse.bass_utils import run_bass_kernel_spmd

    a = {k: np.asarray(v) for k, v in inputs.items()}
    l0, l1 = "L0_conv_", "L1_conv_"

    n = np.arange(C)
    consts = np.concatenate([
        np.eye(C) - 1.0 / C,
        (n[:, None] // GROUP == n[None, :] // GROUP) / GROUP,
        np.eye(C),
    ], axis=1).astype(np.float32)

    arrays = {
        "x": a["x"].reshape(IMAGES, C, PIXELS),
        "consts": consts,
        "vecs": np.stack([a[l0 + v] for v in ("ln0_g", "ln0_b", "ln1_g", "ln1_b", "ln2_g", "ln2_b")], axis=1),
        "w_whiten": a[l0 + "W_whiten"],
        "w_key_t": a[l0 + "W_key"].T,
        "w_recep_t": a[l0 + "W_recep"].T,
        "w_value_t": a[l0 + "W_value"].T,
        "w_out_t": a[l0 + "W_out"].T,
        "w_qkv_t": np.concatenate([a[l1 + w].T for w in ("Wq", "Wk", "Wv")], axis=1),
        "b_t": np.concatenate([a[l1 + "B"].T] * 2, axis=0),
        "w_m_t": np.concatenate([a[l1 + "Wm"].T] * 2, axis=0),
    }
    arrays = {k: np.ascontiguousarray(v) for k, v in arrays.items()}

    nc = bacc.Bacc("TRN2", target_bir_lowering=False, num_devices=1)
    args = [nc.dram_tensor(k, v.shape, mybir.dt.from_np(v.dtype), kind="ExternalInput").ap()
            for k, v in arrays.items()]
    out = nc.dram_tensor("out", (IMAGES, C, PIXELS), F32, kind="ExternalOutput").ap()
    preact_kernel(nc, *args, out)
    r = run_bass_kernel_spmd(nc, [arrays], core_ids=[0])
    return r.results[0]["out"].reshape(IMAGES, C, 128, 128)
```

```python
from contextlib import ExitStack

import numpy as np

import concourse.bass as bass
from concourse import mybir

F32 = mybir.dt.float32
F32R = mybir.dt.float32r
ALU = mybir.AluOpType
ACT = mybir.ActivationFunctionType

C = 128
IMAGES = 4
PIXELS = 128 * 128
TILE = 512
TILES = PIXELS // TILE
ALL = IMAGES * TILES
PIECES = TILE // C
HID = 512
HJ = HID // C
IC = C // 2
PAIRS = TILES // 2
GROUP = C // 32
EPS = 1e-5
CHUNKS = 8
CHUNK = PIXELS // CHUNKS
LAG = 6
LAG_1 = 3
HEAD = 8
UNROLL = 3
LOOPS = (TILES - HEAD) // UNROLL
AHEAD = TILES // LOOPS
assert HEAD + LOOPS * UNROLL == TILES and AHEAD * TILE == CHUNK


def piece(i):
    return slice(i * C, (i + 1) * C)


def preact_kernel(nc, x, consts, vecs, w_whiten, w_key_t, w_recep_t, w_value_t, w_out_t,
                  w_qkv_t, b_t, w_m_t, out):
    with ExitStack() as ctx:
        def sb(name, cols, dtype=F32):
            return ctx.enter_context(nc.sbuf_tensor(name, [C, cols], dtype))

        def sbs(names, cols):
            return [sb(n, cols) for n in names.split()]

        def sems(names):
            return [ctx.enter_context(nc.semaphore(n)) for n in names.split()]

        xs = sb("xs", 2 * PIXELS)

        cst = sb("cst", 2 * C)
        group_mean, ident = cst[:, piece(0)], cst[:, piece(1)]
        vec = sb("vec", 6)
        g0, b0, g1, b1, g2, b2 = (vec[:, i:i + 1] for i in range(6))
        vec_2 = sb("vec_2", 2)
        two_g0, two_b0 = vec_2[:, 0:1], vec_2[:, 1:2]
        whiten, recep_t, out_t, wm_t, exp_b = sbs("whiten recep_t out_t wm_t exp_b", C)
        key_t = sb("key_t", HID)
        value_t = sb("value_t", HJ * C)
        qkv_t = sb("qkv_t", 3 * IC)
        bt = sb("bt", IC)
        two_out_t = sb("two_out_t", C)
        raw_kr = sb("raw_kr", HID + C)
        wkr = sb("wkr", HID + C)
        wkr_hi, wkr_lo = sb("wkr_hi", HID + C, F32R), sb("wkr_lo", HID + C, F32R)
        bias_kr = sb("bias_kr", HJ + 1)
        half_bias_r = sb("half_bias_r", 1)

        gn_in, gn_out = sbs("gn_in gn_out", TILES * 6)
        gn_mv = sb("gn_mv", 2)
        gn_tmp = sb("gn_tmp", 4)
        gain_in, shift_in, gain_out, shift_out, scratch = sbs("gain_in shift_in gain_out shift_out scratch", 1)
        minus_half = sb("minus_half", PIECES)

        gx, t0, t0_kept, s, t1, th, ff = sbs("gx t0 t0_kept s t1 th ff", TILE)
        z_hi, z_lo = sb("z_hi", TILE, F32R), sb("z_lo", TILE, F32R)
        normed = sbs("normed0 normed1 normed2", TILE)
        kk = sb("kk", HJ * TILE)
        halves = sbs("halves0 halves1 halves2", PIECES * 6)
        total = sbs("total0 total1 total2", PIECES)
        apart, within, between = sbs("apart within between", PIECES)
        var = sbs("var0 var1 var2", PIECES)
        rstd = sbs("rstd0 rstd1 rstd2", PIECES)
        shift = sbs("shift0 shift1 shift2", PIECES)

        e, vs, qs, ev, rec, ratio, o = sbs("e vs qs ev rec ratio o", TILE)
        hx = sbs("hx0 hx1", TILE)
        ys = sbs("ys0 ys1", TILE)

        bank = [ctx.enter_context(nc.psum_tensor(f"bank{i}", [C, TILE], F32)) for i in range(8)]
        small = bank[7]

        first_loaded = sems(" ".join(f"first_loaded{i}" for i in range(CHUNKS)))
        weights_loaded, x_loaded, stored = sems("weights_loaded x_loaded stored")
        consts_set, setup_pe, setup_dve, exp_b_ready = sems("consts_set setup_pe setup_dve exp_b_ready")
        gn_pe, gn_dve, gn_gain, in_stats, x1_stats = sems("gn_pe gn_dve gn_gain in_stats x1_stats")

        gx_ready, t0_ready, t0_kept_ready, silu_ready, t1_ready, acc_ready, z_hi_ready, z_lo_ready = sems(
            "gx_ready t0_ready t0_kept_ready silu_ready t1_ready acc_ready z_hi_ready z_lo_ready")
        pix_done = sems("pix0_done pix1_done pix2_done")
        halves_ready = sems("halves0_ready halves1_ready halves2_ready")
        apart_ready = sems("apart0_ready apart1_ready apart2_ready")
        between_ready = sems("between0_ready between1_ready between2_ready")
        var_ready = sems("var0_ready var1_ready var2_ready")
        rstd_ready = sems("rstd0_ready rstd1_ready rstd2_ready")
        shift_ready = sems("shift0_ready shift1_ready shift2_ready")
        normed_ready = sems("normed0_ready normed1_ready normed2_ready")
        back_done = sems("back0_done back1_done back2_done")
        w_done, k_done, r_done, v_done = sems("w_done k_done r_done v_done")
        relu_ready, k_ready, tanh_ready, ff_ready, x1_ready = sems("relu_ready k_ready tanh_ready ff_ready x1_ready")

        hx_ready, kb_done, vb_done, qb_done, den_done, num_done, ob_done = sems(
            "hx_ready kb_done vb_done qb_done den_done num_done ob_done")
        e_ready, vs_ready, qs_ready, ev_ready, rec_ready, ratio_ready, o_ready, ys_ready, y_ready = sems(
            "e_ready vs_ready qs_ready ev_ready rec_ready ratio_ready o_ready ys_ready y_ready")

        GN_DVE, GN_PE = 6, 2

        def norms_before(b, which):
            if which == 0:
                return max(2 * b - 1, 0) if isinstance(b, int) else b * 2 - 1
            if isinstance(b, int):
                return min(2 * b + 2, 2 * IMAGES - 1)
            return b * 2 + 2

        class Step:

            def __init__(self, b, t, loop=None, u=None, ahead=False):
                self.b, self.t, self.loop, self.u, self.ahead = b, t, loop, u, ahead
                self.g = b * TILES + t

            def on(self, lag):
                return not isinstance(self.g, int) or lag <= self.g < ALL + lag

            def n(self, lag):
                return self.g - lag

            def place(self, lag):
                if isinstance(self.t, int) and self.t < lag:
                    return self.b + 1, self.t - lag + TILES
                return self.b, self.t - lag

            def wait(self, eng, sem_, count, each=1):
                if isinstance(count, int):
                    if count <= 0:
                        return
                    count = min(count, ALL)
                eng.wait_ge(sem_, count * each)

        def tile_at(b, t):
            return xs[:, bass.ds((b % 2) * PIXELS + t * TILE, TILE)]

        def run(eng, norm_in, norm_out, step, layer_1):
            def loop(b, ahead):
                with eng.Fori(0, LOOPS) as i:
                    for u in range(UNROLL):
                        step(Step(b, i * UNROLL + HEAD + u, i, u, ahead))

            def image(b, ahead):
                norm_in(b)
                for t in range(HEAD):
                    if t == LAG:
                        norm_out(b - 1)
                    step(Step(b, t))
                layer_1(b - 1)
                loop(b, ahead)

            norm_in(0)
            for t in range(HEAD):
                step(Step(0, t))
            loop(0, True)
            with eng.Fori(1, IMAGES - 1) as b:
                image(b, True)
            image(IMAGES - 1, False)
            for t in range(LAG):
                step(Step(IMAGES, t))
            norm_out(IMAGES - 1)
            layer_1(IMAGES - 1)

        def pair_steps(eng):
            yield from range(LAG_1)
            with eng.Fori(LAG_1, PAIRS) as p:
                yield p
            yield from range(PAIRS, PAIRS + LAG_1)

        def pair_on(p, lag):
            return not isinstance(p, int) or lag <= p < PAIRS + lag

        def pair_wait(eng, sem_, b, count, each=1):
            if not isinstance(count, int) or count > 0:
                eng.wait_ge(sem_, (b * PAIRS + count) * each)

        SETUP = 10

        block = ctx.enter_context(nc.Block())

        @block.sync
        def _(sp):
            for dst, src in ((cst, consts), (vec, vecs)):
                sp.dma_start(dst[:, :], src).then_inc(weights_loaded, 16)
            for i in range(CHUNKS):
                at = slice(i * CHUNK, (i + 1) * CHUNK)
                sp.dma_start(xs[:, at], x[0, :, at]).then_inc(first_loaded[i], 16)
            for dst, src in ((whiten, w_whiten), (key_t, w_key_t), (recep_t, w_recep_t), (out_t, w_out_t),
                             (qkv_t, w_qkv_t), (bt, b_t), (wm_t, w_m_t)):
                sp.dma_start(dst[:, :], src).then_inc(weights_loaded, 16)
            sp.dma_start(value_t[:, :].rearrange("p (j c) -> p j c", j=HJ),
                         w_value_t.rearrange("(j p) c -> p j c", p=C)).then_inc(weights_loaded, 16)

            def columns(b, i):
                return xs[:, bass.ds((b % 2) * PIXELS + i * CHUNK, CHUNK)]

            def load(b, i):
                sp.dma_start(columns(b, i), x[b, :, bass.ts(i, CHUNK)]).then_inc(x_loaded, 16)

            def store(b, i):
                sp.wait_ge(y_ready, b * TILES + (i + 1) * (TILES // CHUNKS))
                sp.dma_start(out[b, :, bass.ts(i, CHUNK)], columns(b, i)).then_inc(stored, 16)

            load(1, 0)
            with sp.Fori(1, CHUNKS) as i:
                sp.wait_ge(x_loaded, i * 16)
                load(1, i)
            with sp.Fori(0, IMAGES - 2) as b:
                store(b, 0)
                with sp.Fori(1, CHUNKS) as i:
                    sp.wait_ge(stored, (b * CHUNKS + i) * 16)
                    sp.wait_ge(x_loaded, ((b + 1) * CHUNKS + i - 1) * 16)
                    load(b + 2, i - 1)
                    store(b, i)
                sp.wait_ge(stored, (b + 1) * CHUNKS * 16)
                sp.wait_ge(x_loaded, ((b + 2) * CHUNKS - 1) * 16)
                load(b + 2, CHUNKS - 1)
            with sp.Fori(IMAGES - 2, IMAGES) as b:
                with sp.Fori(0, CHUNKS) as i:
                    store(b, i)
            sp.wait_ge(stored, IMAGES * CHUNKS * 16)

        @block.tensor
        def _(pe):
            mm = nc.tensor.matmul

            def one(dst, lhs, rhs):
                return mm(dst, lhs, rhs, start=True, stop=True)

            def transpose_pieces(dst, src):
                for i in range(PIECES):
                    last = nc.tensor.transpose(dst[:, piece(i)], src[:, piece(i)], ident)
                return last

            pe.wait_ge(weights_loaded, 10 * 16)
            one(bank[0][:, :], whiten[:, :], key_t[:, :])
            one(bank[1][:, 0:C], whiten[:, :], recep_t[:, :]).then_inc(setup_pe, 1)
            pe.wait_ge(setup_dve, 4)
            for j in range(HJ + 1):
                last = one(bank[2][:, j:j + 1], raw_kr[:, piece(j)], b2)
            last.then_inc(setup_pe, 1)

            def group_norm(b, which):
                n = norms_before(b, which) * GN_DVE
                pe.wait_ge(gn_dve, n + 1)
                one(small[:, 0:1], group_mean, gn_mv[:, 0:1]).then_inc(gn_pe, 1)
                pe.wait_ge(gn_dve, n + 4)
                one(small[:, 1:2], group_mean, gn_tmp[:, 2:3]).then_inc(gn_pe, 1)
                pe.wait_ge(gn_dve, n + 6)

            def norm_in(b):
                if not isinstance(b, int) or b:
                    pe.wait_ge(z_lo_ready, b * TILES - 3)
                group_norm(b, 0)
                pe.wait_ge(setup_dve, SETUP)

            def norm_out(b):
                st = Step(IMAGES, LAG) if isinstance(b, int) and b == IMAGES - 1 else Step(b + 1, LAG)
                st.wait(pe, z_lo_ready, st.n(3))
                group_norm(b, 1)

            def step(st):
                def need(sem_, count):
                    st.wait(pe, sem_, count)

                n0, n1, n2, n3, n4, n5 = (st.n(i) for i in range(6))

                def product(dst, w):
                    mm(dst, wkr_hi[:, w], z_hi[:, :], start=True, stop=False)
                    mm(dst, wkr_lo[:, w], z_hi[:, :], start=False, stop=False)
                    return mm(dst, wkr_hi[:, w], z_lo[:, :], start=False, stop=True)

                def keys(j):
                    if st.on(4):
                        if j == 0:
                            need(z_lo_ready, n4 + 1)
                        count = n4 * HJ + j - 1
                        if not isinstance(count, int) or count > 0:
                            pe.wait_ge(relu_ready, count)
                        product(bank[3 + j % 2][:, :], piece(j)).then_inc(k_done, 1)

                def values(j, lag):
                    if st.on(lag):
                        if j == 0:
                            need(ff_ready, st.n(lag))
                        pe.wait_ge(k_ready, st.n(lag) * HJ + j + 1)
                        mm(bank[5][:, :], value_t[:, piece(j)], kk[:, j * TILE:(j + 1) * TILE],
                           start=(j == 0), stop=(j == HJ - 1)).then_inc(v_done, 1)

                if st.u == 0 and not (isinstance(st.b, int) and st.b == 0):
                    pe.wait_ge(ys_ready, st.b * TILES)
                values(1, 5)
                values(2, 5)
                if st.on(3):
                    need(t1_ready, n3 + 1)
                    need(normed_ready[2], n3)
                    transpose_pieces(bank[2], t1).then_inc(pix_done[2], 1)
                keys(0)
                if st.on(1):
                    need(normed_ready[0], n1 + 1)
                    need(z_lo_ready, n3)
                    transpose_pieces(bank[7], normed[0]).then_inc(back_done[0], 1)
                values(3, 5)
                keys(1)
                keys(2)
                if st.on(4):
                    need(t1_ready, n2)
                    product(bank[6][:, :], piece(HJ)).then_inc(r_done, 1)
                if st.on(0):
                    need(gx_ready, n0 + 1)
                    need(normed_ready[0], n0)
                    transpose_pieces(bank[0], gx).then_inc(pix_done[0], 1)
                if st.on(1):
                    need(t0_ready, n1 + 1)
                    need(normed_ready[1], n1)
                    transpose_pieces(bank[1], t0).then_inc(pix_done[1], 1)
                keys(3)
                if st.on(2):
                    need(normed_ready[1], n2 + 1)
                    need(t1_ready, n2)
                    need(tanh_ready, n4 + 1)
                    transpose_pieces(bank[6], normed[1]).then_inc(back_done[1], 1)
                values(0, 4)
                if st.on(3):
                    need(normed_ready[2], n3 + 1)
                    need(t0_ready, n1 + 1)
                    transpose_pieces(bank[7], normed[2]).then_inc(back_done[2], 1)
                if st.on(2):
                    need(silu_ready, n2 + 1)
                    one(bank[6][:, :], two_out_t[:, :], s[:, :]).then_inc(w_done, 1)

            def layer_1(b):
                st = Step(b + 1, HEAD - 1) if not isinstance(b, int) or b < IMAGES - 1 else Step(IMAGES, LAG - 1)
                st.wait(pe, normed_ready[0], st.n(0) + 1)
                st.wait(pe, normed_ready[1], st.n(1) + 1)
                st.wait(pe, normed_ready[2], st.n(3) + 1)
                st.wait(pe, relu_ready, st.n(4) + 1, HJ)
                st.wait(pe, tanh_ready, st.n(4) + 1)
                st.wait(pe, t1_ready, st.n(2) + 1)
                st.wait(pe, z_lo_ready, st.n(3) + 1)

                def need(sem_, count, each=1):
                    pair_wait(pe, sem_, b, count, each)

                def project(dst, which):
                    w = qkv_t[:, which * IC:(which + 1) * IC]
                    one(dst[0:IC, :], w, hx[0][:, :])
                    return one(dst[IC:C, :], w, hx[1][:, :])

                for p in pair_steps(pe):
                    if pair_on(p, 1):
                        need(hx_ready, p, 2)
                        need(e_ready, p - 1)
                        project(bank[0], 1).then_inc(kb_done, 1)
                        need(vs_ready, p - 1)
                        project(bank[1], 2).then_inc(vb_done, 1)
                        need(qs_ready, p - 1)
                        project(bank[4], 0).then_inc(qb_done, 1)
                    if pair_on(p, 2):
                        need(e_ready, p - 1)
                        need(rec_ready, p - 2)
                        one(bank[2][:, :], exp_b[:, :], e[:, :]).then_inc(den_done, 1)
                        need(ev_ready, p - 1)
                        need(ratio_ready, p - 2)
                        one(bank[3][:, :], exp_b[:, :], ev[:, :]).then_inc(num_done, 1)
                    if pair_on(p, 3):
                        need(o_ready, p - 2)
                        need(ys_ready, p - 3, 2)
                        one(bank[6][:, :], wm_t[0:IC, :], o[0:IC, :])
                        one(bank[7][:, :], wm_t[IC:C, :], o[IC:C, :]).then_inc(ob_done, 1)

            run(pe, norm_in, norm_out, step, layer_1)

        @block.scalar
        def _(act):
            f = nc.scalar.activation
            act.wait_ge(consts_set, 2)
            act.wait_ge(weights_loaded, 10 * 16)
            for h in range(2):
                q = slice(h * IC, (h + 1) * IC)
                last = f(exp_b[q, q], bt[q, :], ACT.Exp)
            last.then_inc(exp_b_ready, 1)
            act.wait_ge(setup_dve, SETUP)

            def no_norm(b):
                pass

            def step(st):
                def need(sem_, count, each=1):
                    st.wait(act, sem_, count, each)

                n0, n1, n2, n3, n4 = (st.n(i) for i in range(5))

                def relu(j):
                    if st.on(4):
                        count = (n4 - 1) * HJ + j + 1
                        if not isinstance(count, int) or count > 0:
                            act.wait_ge(v_done, count)
                        act.wait_ge(k_done, n4 * HJ + j + 1)
                        f(kk[:, j * TILE:(j + 1) * TILE], bank[3 + j % 2][:, :], ACT.Relu,
                          bias=bias_kr[:, j:j + 1]).then_inc(relu_ready, 1)

                def norm(i, lag):
                    if not st.on(lag):
                        return
                    n = st.n(lag)
                    need(shift_ready[i], n + 1)
                    need(back_done[i], n)
                    for q in range(PIECES):
                        last = f(normed[i][:, piece(q)], bank[i][:, piece(q)], ACT.Identity,
                                 bias=shift[i][:, q:q + 1], scale=rstd[i][:, q:q + 1])
                    last.then_inc(normed_ready[i], 1)

                relu(0)
                if st.on(1):
                    need(back_done[0], n1 + 1)
                    need(pix_done[1], n1)
                    need(t0_kept_ready, n1)
                    f(t0[:, :], bank[7][:, :], ACT.Identity, bias=two_b0, scale=two_g0).then_inc(t0_ready, 1)
                relu(1)
                relu(2)
                if st.on(4):
                    need(r_done, n4 + 1)
                    need(ff_ready, n4)
                    f(th[:, :], bank[6][:, :], ACT.Tanh, bias=half_bias_r[:, :], scale=0.5).then_inc(tanh_ready, 1)
                norm(2, 3)
                if st.on(2):
                    need(back_done[1], n2 + 1)
                    need(w_done, n2)
                    f(s[:, :], bank[6][:, :], ACT.Silu, bias=b1, scale=g1).then_inc(silu_ready, 1)
                relu(3)
                if st.on(3):
                    need(back_done[2], n3 + 1)
                    need(k_done, n3, HJ)
                    f(z_hi[:, :], bank[7][:, :], ACT.Copy).then_inc(z_hi_ready, 1)
                norm(0, 0)
                norm(1, 1)

            def layer_1(b):
                act.wait_ge(gn_dve, (norms_before(b, 1) + 1) * GN_DVE)

                def need(sem_, count, each=1):
                    pair_wait(act, sem_, b, count, each)

                for p in pair_steps(act):
                    if pair_on(p, 1):
                        need(kb_done, p)
                        need(den_done, p - 1)
                        need(ev_ready, p - 1)
                        f(e[:, :], bank[0][:, :], ACT.Exp).then_inc(e_ready, 1)
                        need(vb_done, p)
                        f(vs[:, :], bank[1][:, :], ACT.Copy).then_inc(vs_ready, 1)
                    if pair_on(p, 0):
                        need(qb_done, p)
                        for h in range(2):
                            f(hx[h][:, :], tile_at(b, p * 2 + h), ACT.Identity, bias=shift_out[:, :],
                              scale=gain_out[:, :]).then_inc(hx_ready, 1)
                    if pair_on(p, 3):
                        need(ob_done, p - 2)
                        need(y_ready, p - 3, 2)
                        for h in range(2):
                            f(ys[h][:, :], bank[6 + h][:, :], ACT.Copy).then_inc(ys_ready, 1)
                    if pair_on(p, 1):
                        need(qb_done, p)
                        need(o_ready, p - 1)
                        f(qs[:, :], bank[4][:, :], ACT.Copy).then_inc(qs_ready, 1)

            run(act, no_norm, no_norm, step, layer_1)

        @block.gpsimd
        def _(pool):
            tt = nc.gpsimd.tensor_tensor
            nc.gpsimd.memset(minus_half[:, :], -0.5).then_inc(consts_set, 1)
            nc.gpsimd.memset(exp_b[:, :], 0.0).then_inc(consts_set, 1)
            pool.wait_ge(consts_set, 2)

            def group_norm(b, which, gain):
                pool.wait_ge(gn_dve, norms_before(b, which) * GN_DVE + 5)
                tt(gain[:, :], gn_tmp[:, 3:4], minus_half[:, 0:1], ALU.pow).then_inc(gn_gain, 1)

            def norm_in(b):
                group_norm(b, 0, gain_in)

            def step(st):
                def need(sem_, count):
                    st.wait(pool, sem_, count)

                n3 = st.n(3)

                def square(j, lag):
                    if st.on(lag):
                        pool.wait_ge(relu_ready, st.n(lag) * HJ + j + 1)
                        k = kk[:, j * TILE:(j + 1) * TILE]
                        tt(k, k, k, ALU.mult).then_inc(k_ready, 1)

                def rsqrt(i, lag):
                    if st.on(lag):
                        need(var_ready[i], st.n(lag) + 1)
                        need(normed_ready[i], st.n(lag))
                        tt(rstd[i][:, :], var[i][:, :], minus_half[:, :], ALU.pow).then_inc(rstd_ready[i], 1)

                square(3, 5)
                if st.on(3):
                    need(t1_ready, n3 + 1)
                    acc = tile_at(*st.place(3))
                    tt(acc, acc, t1[:, :], ALU.add).then_inc(acc_ready, 1)
                rsqrt(2, 3)
                square(0, 4)
                square(1, 4)
                square(2, 4)
                rsqrt(0, 0)
                rsqrt(1, 1)

            def norm_out(b):
                group_norm(b, 1, gain_out)

            def layer_1(b):

                def need(sem_, count, each=1):
                    pair_wait(pool, sem_, b, count, each)

                for p in pair_steps(pool):
                    if pair_on(p, 1):
                        need(vs_ready, p)
                        need(e_ready, p)
                        need(num_done, p - 1)
                        tt(ev[:, :], e[:, :], vs[:, :], ALU.mult).then_inc(ev_ready, 1)
                    if pair_on(p, 3):
                        for h in range(2):
                            pool.wait_ge(ys_ready, b * TILES + (p - 3) * 2 + h + 1)
                            y = tile_at(b, (p - 3) * 2 + h)
                            tt(y, y, ys[h][:, :], ALU.add).then_inc(y_ready, 1)

            run(pool, norm_in, norm_out, step, layer_1)

        @block.vector
        def _(dve):
            v = nc.vector
            dve.wait_ge(weights_loaded, 10 * 16)
            v.tensor_scalar(two_out_t[:, :], out_t[:, :], 2.0, None, ALU.mult).then_inc(setup_dve, 1)
            v.tensor_scalar(vec_2[:, :], vec[:, 0:2], 2.0, None, ALU.mult).then_inc(setup_dve, 1)
            dve.wait_ge(setup_pe, 1)
            v.tensor_copy(raw_kr[:, 0:HID], bank[0][:, :]).then_inc(setup_dve, 1)
            v.tensor_copy(raw_kr[:, HID:HID + C], bank[1][:, 0:C]).then_inc(setup_dve, 1)
            dve.wait_ge(setup_dve, 4)
            v.tensor_scalar(wkr[:, :], raw_kr[:, :], g2, None, ALU.mult).then_inc(setup_dve, 1)
            dve.wait_ge(setup_pe, 2)
            v.tensor_copy(bias_kr[:, :], bank[2][:, 0:HJ + 1]).then_inc(setup_dve, 1)
            v.tensor_scalar(half_bias_r[:, :], bank[2][:, HJ:HJ + 1], 0.5, None, ALU.mult).then_inc(setup_dve, 1)
            dve.wait_ge(setup_dve, 5)
            v.tensor_copy(wkr_hi[:, :], wkr[:, :]).then_inc(setup_dve, 1)
            dve.wait_ge(setup_dve, 8)
            v.tensor_tensor(wkr_lo[:, :], wkr[:, :], wkr_hi[:, :], ALU.subtract).then_inc(setup_dve, 1)
            dve.wait_ge(exp_b_ready, 1)
            v.memset(scratch[:, :], 0.0).then_inc(setup_dve, 1)

            for t in range(TILES):
                if t % (TILES // CHUNKS) == 0:
                    dve.wait_ge(first_loaded[t // (TILES // CHUNKS)], 16)
                v.bn_stats(gn_in[:, t * 6:(t + 1) * 6], xs[:, t * TILE:(t + 1) * TILE]).then_inc(in_stats, 1)

            def group_norm(b, which, stats, gain, shift_):
                n = norms_before(b, which)

                def done(k):
                    dve.wait_ge(gn_dve, n * GN_DVE + k)

                mean, channel_var = gn_mv[:, 0:1], gn_mv[:, 1:2]
                off, off2, about, group_var = (gn_tmp[:, i:i + 1] for i in range(4))
                v.memset(scratch[:, :], 0.0)
                v.bn_aggr(gn_mv[:, :], stats[:, :]).then_inc(gn_dve, 1)
                dve.wait_ge(gn_pe, n * GN_PE + 1)
                v.tensor_tensor(off, mean, small[:, 0:1], ALU.subtract).then_inc(gn_dve, 1)
                done(2)
                v.tensor_tensor(off2, off, off, ALU.mult).then_inc(gn_dve, 1)
                done(3)
                v.tensor_tensor(about, channel_var, off2, ALU.add).then_inc(gn_dve, 1)
                dve.wait_ge(gn_pe, n * GN_PE + 2)
                v.tensor_scalar(group_var, small[:, 1:2], EPS, None, ALU.add).then_inc(gn_dve, 1)
                dve.wait_ge(gn_gain, n + 1)
                v.scalar_tensor_tensor(out=shift_[:, :], in0=small[:, 0:1], scalar=-1.0, in1=gain[:, :],
                                       op0=ALU.mult, op1=ALU.mult).then_inc(gn_dve, 1)
                done(6)

            def norm_in(b):
                dve.wait_ge(in_stats, (b + 1) * TILES)
                group_norm(b, 0, gn_in, gain_in, shift_in)

            def step(st):
                def need(sem_, count, each=1):
                    st.wait(dve, sem_, count, each)

                n0, n1, n2, n3, n4, n5, n6 = (st.n(i) for i in range(7))

                def moments(i, lag, epsilon):
                    if not st.on(lag):
                        return
                    n = st.n(lag)
                    h = halves[i]
                    need(pix_done[i], n + 1)
                    for q in range(PIECES):
                        last = v.bn_stats(h[:, q * 6:(q + 1) * 6], bank[i][:, piece(q)])
                    last.then_inc(halves_ready[i], 1)
                    need(halves_ready[i], n + 1)
                    v.tensor_tensor(apart[:, :], h[:, 1::6], h[:, 4::6], ALU.subtract).then_inc(apart_ready[i], 1)
                    v.tensor_tensor(total[i][:, :], h[:, 1::6], h[:, 4::6], ALU.add)
                    v.scalar_tensor_tensor(out=within[:, :], in0=h[:, 2::6], scalar=C * epsilon, in1=h[:, 5::6],
                                           op0=ALU.add, op1=ALU.add)
                    need(apart_ready[i], n + 1)
                    v.scalar_tensor_tensor(out=between[:, :], in0=apart[:, :], scalar=0.25, in1=apart[:, :],
                                           op0=ALU.mult, op1=ALU.mult).then_inc(between_ready[i], 1)
                    need(between_ready[i], n + 1)
                    v.scalar_tensor_tensor(out=var[i][:, :], in0=within[:, :], scalar=1.0 / C, in1=between[:, :],
                                           op0=ALU.mult, op1=ALU.add).then_inc(var_ready[i], 1)

                def shifts(i, lag):
                    if st.on(lag):
                        need(rstd_ready[i], st.n(lag) + 1)
                        v.scalar_tensor_tensor(out=shift[i][:, :], in0=total[i][:, :], scalar=-0.5,
                                               in1=rstd[i][:, :], op0=ALU.mult, op1=ALU.mult)\
                         .then_inc(shift_ready[i], 1)

                def next_stats(k):
                    t = st.loop * AHEAD + k
                    v.bn_stats(gn_in[:, bass.ds(t * 6, 6)], tile_at(st.b + 1, t)).then_inc(in_stats, 1)

                if st.on(0):
                    need(pix_done[0], n0)
                    v.tensor_scalar(gx[:, :], tile_at(*st.place(0)), gain_in[:, :], shift_in[:, :],
                                    ALU.mult, ALU.add).then_inc(gx_ready, 1)
                if st.on(2):
                    need(t0_ready, n2 + 1)
                    need(t1_ready, n2)
                    v.tensor_copy(t0_kept[:, :], t0[:, :]).then_inc(t0_kept_ready, 1)
                moments(2, 3, 4 * EPS)
                if st.on(6):
                    need(ff_ready, n6 + 1)
                    need(acc_ready, n6 + 1)
                    x1 = tile_at(*st.place(6))
                    v.tensor_tensor(x1, x1, ff[:, :], ALU.add).then_inc(x1_ready, 1)
                if st.ahead:
                    dve.wait_ge(x_loaded, (st.b * CHUNKS + st.loop + 1) * 16)
                if st.on(5):
                    need(v_done, n5 + 1, HJ)
                    need(tanh_ready, n5 + 1)
                    need(x1_ready, n5)
                    v.scalar_tensor_tensor(out=ff[:, :], in0=th[:, :], scalar=1.0, in1=bank[5][:, :],
                                           op0=ALU.add, op1=ALU.mult).then_inc(ff_ready, 1)
                if st.ahead:
                    next_stats(0 if st.u == 0 else st.u + 1)
                if st.on(6):
                    need(x1_ready, n6 + 1)
                if st.on(3):
                    shifts(2, 3)
                elif st.on(6):
                    v.memset(scratch[:, :], 0.0)
                if st.on(6):
                    slot = st.place(6)[1]
                    v.bn_stats(gn_out[:, bass.ds(slot * 6, 6)], tile_at(*st.place(6))).then_inc(x1_stats, 1)
                moments(0, 0, EPS)
                moments(1, 1, 4 * EPS)
                shifts(0, 0)
                if st.on(2):
                    need(w_done, n2 + 1)
                    need(t0_kept_ready, n2 + 1)
                    need(pix_done[2], n2)
                    need(acc_ready, n2)
                    v.tensor_tensor(t1[:, :], bank[6][:, :], t0_kept[:, :], ALU.add).then_inc(t1_ready, 1)
                if st.on(3):
                    need(z_hi_ready, n3 + 1)
                    v.tensor_tensor(z_lo[:, :], bank[7][:, :], z_hi[:, :], ALU.subtract).then_inc(z_lo_ready, 1)
                shifts(1, 1)
                if st.ahead and st.u == 0:
                    next_stats(1)

            def norm_out(b):
                dve.wait_ge(x1_stats, (b + 1) * TILES)
                group_norm(b, 1, gn_out, gain_out, shift_out)

            def layer_1(b):

                def need(sem_, count, each=1):
                    pair_wait(dve, sem_, b, count, each)

                for p in pair_steps(dve):
                    if pair_on(p, 2):
                        need(den_done, p - 1)
                        need(ratio_ready, p - 2)
                        v.reciprocal(rec[:, :], bank[2][:, :]).then_inc(rec_ready, 1)
                        need(num_done, p - 1)
                        need(rec_ready, p - 1)
                        v.tensor_tensor(ratio[:, :], rec[:, :], bank[3][:, :], ALU.mult).then_inc(ratio_ready, 1)
                        need(qs_ready, p - 1)
                        need(ratio_ready, p - 1)
                        need(ob_done, p - 2)
                        v.tensor_tensor(o[:, :], qs[:, :], ratio[:, :], ALU.mult).then_inc(o_ready, 1)

            run(dve, norm_in, norm_out, step, layer_1)


def kernel(**inputs):
    import concourse.bacc as bacc
    from concourse.bass_utils import run_bass_kernel_spmd

    a = {k: np.asarray(v) for k, v in inputs.items()}
    l0, l1 = "L0_conv_", "L1_conv_"

    n = np.arange(C)
    consts = np.concatenate([
        (n[:, None] // GROUP == n[None, :] // GROUP) / GROUP,
        np.eye(C),
    ], axis=1).astype(np.float32)

    arrays = {
        "x": a["x"].reshape(IMAGES, C, PIXELS),
        "consts": consts,
        "vecs": np.stack([a[l0 + v] for v in ("ln0_g", "ln0_b", "ln1_g", "ln1_b", "ln2_g", "ln2_b")], axis=1),
        "w_whiten": a[l0 + "W_whiten"],
        "w_key_t": a[l0 + "W_key"].T,
        "w_recep_t": a[l0 + "W_recep"].T,
        "w_value_t": a[l0 + "W_value"].T,
        "w_out_t": a[l0 + "W_out"].T,
        "w_qkv_t": np.concatenate([a[l1 + w].T for w in ("Wq", "Wk", "Wv")], axis=1),
        "b_t": np.concatenate([a[l1 + "B"].T] * 2, axis=0),
        "w_m_t": np.concatenate([a[l1 + "Wm"].T] * 2, axis=0),
    }
    arrays = {k: np.ascontiguousarray(v) for k, v in arrays.items()}

    nc = bacc.Bacc("TRN2", target_bir_lowering=False, num_devices=1)
    args = [nc.dram_tensor(k, v.shape, mybir.dt.from_np(v.dtype), kind="ExternalInput").ap()
            for k, v in arrays.items()]
    out = nc.dram_tensor("out", (IMAGES, C, PIXELS), F32, kind="ExternalOutput").ap()
    preact_kernel(nc, *args, out)
    r = run_bass_kernel_spmd(nc, [arrays], core_ids=[0])
    return r.results[0]["out"].reshape(IMAGES, C, 128, 128)
```

```python
from contextlib import ExitStack

import numpy as np

import concourse.bass as bass
from concourse import mybir

F32 = mybir.dt.float32
F32R = mybir.dt.float32r
ALU = mybir.AluOpType
ACT = mybir.ActivationFunctionType

C = 128
IMAGES = 4
PIXELS = 128 * 128
TILE = 512
TILES = PIXELS // TILE
ALL = IMAGES * TILES
PIECES = TILE // C
HID = 512
HJ = HID // C
IC = C // 2
PAIRS = TILES // 2
GROUP = C // 32
EPS = 1e-5
CHUNKS = 8
CHUNK = PIXELS // CHUNKS
LAG = 6
LAG_1 = 4
FILL_1 = 6
UNROLL_1 = 2
HEAD = LAG + 2
UNROLL = 3
LOOPS = (TILES - HEAD) // UNROLL
AHEAD = TILES // LOOPS
assert HEAD + LOOPS * UNROLL == TILES and AHEAD * TILE == CHUNK


def piece(i):
    return slice(i * C, (i + 1) * C)


def preact_kernel(nc, x, consts, vecs, w_whiten, w_key_t, w_recep_t, w_value_t, w_out_t,
                  w_qkv_t, b_t, w_m_t, out):
    with ExitStack() as ctx:
        def sb(name, cols, dtype=F32):
            return ctx.enter_context(nc.sbuf_tensor(name, [C, cols], dtype))

        def sbs(names, cols):
            return [sb(n, cols) for n in names.split()]

        def sems(names):
            return [ctx.enter_context(nc.semaphore(n)) for n in names.split()]

        xs = sb("xs", 2 * PIXELS)

        cst = sb("cst", 2 * C)
        group_mean, ident = cst[:, piece(0)], cst[:, piece(1)]
        vec = sb("vec", 6)
        g0, b0, g1, b1, g2, b2 = (vec[:, i:i + 1] for i in range(6))
        vec_2 = sb("vec_2", 2)
        two_g0, two_b0 = vec_2[:, 0:1], vec_2[:, 1:2]
        wm_t, exp_b = sbs("wm_t exp_b", C)
        wm_hi, wm_lo = sb("wm_hi", C, F32R), sb("wm_lo", C, F32R)
        key_t = sb("key_t", HID)
        value_t = sb("value_t", HJ * C)
        qkv_t = sb("qkv_t", 3 * IC)
        bt = sb("bt", IC)
        two_out_t = sb("two_out_t", C)
        wkr_hi, wkr_lo = sb("wkr_hi", HID + C, F32R), sb("wkr_lo", HID + C, F32R)
        bias_kr = sb("bias_kr", HJ + 1)
        half_bias_r = sb("half_bias_r", 1)

        gn_in, gn_out = sbs("gn_in gn_out", TILES * 6)
        gn_mv = sb("gn_mv", 2)
        gn_tmp = sb("gn_tmp", 5)
        gain_in, shift_in, gain_out, shift_out, scratch = sbs("gain_in shift_in gain_out shift_out scratch", 1)
        minus_half = sb("minus_half", PIECES)

        gx, t0, t0_kept, s, t1, th, ff = sbs("gx t0 t0_kept s t1 th ff", TILE)
        z_hi, z_lo = sb("z_hi", TILE, F32R), sb("z_lo", TILE, F32R)
        normed = sbs("normed0 normed1 normed2", TILE)
        kk = sb("kk", HJ * TILE)
        halves = sbs("halves0 halves1 halves2", PIECES * 6)
        total = sbs("total0 total1 total2", PIECES)
        apart, within, between = sbs("apart within between", PIECES)
        var = sbs("var0 var1 var2", PIECES)
        rstd = sbs("rstd0 rstd1 rstd2", PIECES)
        shift = sbs("shift0 shift1 shift2", PIECES)

        raw_kr, wkr = (kk[:, i * 2 * TILE:i * 2 * TILE + HID + C] for i in range(2))
        whiten, recep_t, out_t = (kk[:, HID + C * i:HID + C * (i + 1)] for i in (1, 2, 3))

        e, vs, qs, ev, rec, ratio, o = sbs("e vs qs ev rec ratio o", TILE)
        o_hi, o_lo = sb("o_hi", TILE, F32R), sb("o_lo", TILE, F32R)
        hx = sbs("hx0 hx1", TILE)
        ys = sbs("ys0 ys1", TILE)

        bank = [ctx.enter_context(nc.psum_tensor(f"bank{i}", [C, TILE], F32)) for i in range(8)]
        small = bank[7]
        k_bank, v_bank, q_bank, den_bank, num_bank = (bank[i] for i in (3, 4, 2, 7, 6))

        first_loaded = sems(" ".join(f"first_loaded{i}" for i in range(CHUNKS)))
        weights_loaded, x_loaded, stored = sems("weights_loaded x_loaded stored")
        consts_set, setup_pe, setup_dve, exp_b_ready = sems("consts_set setup_pe setup_dve exp_b_ready")
        gn_pe, gn_dve, gn_gain, in_stats, x1_stats = sems("gn_pe gn_dve gn_gain in_stats x1_stats")

        gx_ready, t0_ready, t0_kept_ready, silu_ready, t1_ready, acc_ready, z_hi_ready, z_lo_ready = sems(
            "gx_ready t0_ready t0_kept_ready silu_ready t1_ready acc_ready z_hi_ready z_lo_ready")
        pix_done = sems("pix0_done pix1_done pix2_done")
        halves_ready = sems("halves0_ready halves1_ready halves2_ready")
        apart_ready = sems("apart0_ready apart1_ready apart2_ready")
        between_ready = sems("between0_ready between1_ready between2_ready")
        var_ready = sems("var0_ready var1_ready var2_ready")
        rstd_ready = sems("rstd0_ready rstd1_ready rstd2_ready")
        shift_ready = sems("shift0_ready shift1_ready shift2_ready")
        normed_ready = sems("normed0_ready normed1_ready normed2_ready")
        back_done = sems("back0_done back1_done back2_done")
        w_done, k_done, r_done, v_done = sems("w_done k_done r_done v_done")
        relu_ready, k_ready, tanh_ready, ff_ready, x1_ready = sems("relu_ready k_ready tanh_ready ff_ready x1_ready")

        o_hi_ready, o_lo_ready = sems("o_hi_ready o_lo_ready")
        hx_ready, kb_done, vb_done, qb_done, den_done, num_done, ob_done = sems(
            "hx_ready kb_done vb_done qb_done den_done num_done ob_done")
        e_ready, vs_ready, qs_ready, ev_ready, rec_ready, ratio_ready, o_ready, ys_ready, y_ready = sems(
            "e_ready vs_ready qs_ready ev_ready rec_ready ratio_ready o_ready ys_ready y_ready")

        GN_DVE, GN_PE = 7, 2

        def norms_before(b, which):
            if which == 0:
                return max(2 * b - 1, 0) if isinstance(b, int) else b * 2 - 1
            if isinstance(b, int):
                return min(2 * b + 2, 2 * IMAGES - 1)
            return b * 2 + 2

        class Step:

            def __init__(self, b, t, loop=None, u=None, ahead=False, norm=None):
                self.b, self.t = b, t
                self.loop, self.u = loop, u
                self.ahead = ahead
                self.behind_layer_1 = loop is not None and isinstance(t, int) and t == HEAD \
                    and not (isinstance(b, int) and b == 0)
                self.starts_layer_1 = loop is None and t == HEAD - 1 and not (isinstance(b, int) and b == 0)
                self.norm = norm or (None, None, None)
                self.g = b * TILES + t

            def on(self, lag):
                return not isinstance(self.g, int) or lag <= self.g < ALL + lag

            def n(self, lag):
                return self.g - lag

            def place(self, lag):
                if isinstance(self.t, int) and self.t < lag:
                    return self.b + 1, self.t - lag + TILES
                return self.b, self.t - lag

            def wait(self, eng, sem_, count, each=1):
                if isinstance(count, int):
                    if count <= 0:
                        return
                    count = min(count, ALL)
                eng.wait_ge(sem_, count * each)

        def tile_at(b, t):
            return xs[:, bass.ds((b % 2) * PIXELS + t * TILE, TILE)]

        def run(eng, whole_norm, step, layer_1):
            def loop(b, ahead):
                for u in range(UNROLL):
                    step(Step(b, HEAD + u, 0, u, ahead))
                with eng.Fori(1, LOOPS - 1) as i:
                    for u in range(UNROLL):
                        step(Step(b, i * UNROLL + HEAD + u, i, u, ahead))
                for u in range(UNROLL):
                    norm = (b + 1, 0, u) if ahead and u > 0 else None
                    step(Step(b, TILES - UNROLL + u, LOOPS - 1, u, ahead, norm))

            def image(b, ahead):
                for t in range(HEAD):
                    step(Step(b, t, norm=(b - 1, 1, t - LAG + 2) if LAG - 1 <= t <= LAG else None))
                layer_1(b - 1)
                loop(b, ahead)

            whole_norm(0, 0)
            for t in range(HEAD):
                step(Step(0, t))
            loop(0, True)
            with eng.Fori(1, IMAGES - 1) as b:
                image(b, True)
            image(IMAGES - 1, False)
            for t in range(LAG):
                step(Step(IMAGES, t))
            whole_norm(IMAGES - 1, 1)
            layer_1(IMAGES - 1)

        def pair_steps(eng):
            yield from range(FILL_1)
            with eng.Fori(0, (PAIRS - FILL_1) // UNROLL_1) as i:
                for u in range(UNROLL_1):
                    yield i * UNROLL_1 + FILL_1 + u
            yield from range(PAIRS, PAIRS + LAG_1)

        def pair_on(p, lag):
            return not isinstance(p, int) or lag <= p < PAIRS + lag

        def pair_wait(eng, sem_, b, count, each=1):
            if not isinstance(count, int) or count > 0:
                eng.wait_ge(sem_, b * PAIRS * each + count)

        SETUP = 12

        block = ctx.enter_context(nc.Block())

        @block.sync
        def _(sp):
            def first_load(i):
                at = slice(i * CHUNK, (i + 1) * CHUNK)
                sp.dma_start(xs[:, at], x[0, :, at]).then_inc(first_loaded[i], 16)

            first_load(0)
            first_load(1)
            for dst, src in ((cst, consts), (vec, vecs), (whiten, w_whiten), (key_t, w_key_t), (recep_t, w_recep_t), (out_t, w_out_t),
                             (qkv_t, w_qkv_t), (bt, b_t), (wm_t, w_m_t)):
                sp.dma_start(dst[:, :], src).then_inc(weights_loaded, 16)
            sp.dma_start(value_t[:, :].rearrange("p (j c) -> p j c", j=HJ),
                         w_value_t.rearrange("(j p) c -> p j c", p=C)).then_inc(weights_loaded, 16)
            for i in range(2, CHUNKS):
                first_load(i)

            def columns(b, i):
                return xs[:, bass.ds((b % 2) * PIXELS + i * CHUNK, CHUNK)]

            def load(b, i):
                sp.dma_start(columns(b, i), x[b, :, bass.ts(i, CHUNK)]).then_inc(x_loaded, 16)

            def store(b, i):
                sp.wait_ge(y_ready, b * TILES + (i + 1) * (TILES // CHUNKS))
                sp.dma_start(out[b, :, bass.ts(i, CHUNK)], columns(b, i)).then_inc(stored, 16)

            load(1, 0)
            with sp.Fori(1, CHUNKS) as i:
                sp.wait_ge(x_loaded, i * 16)
                load(1, i)
            with sp.Fori(0, IMAGES - 2) as b:
                store(b, 0)
                with sp.Fori(1, CHUNKS) as i:
                    sp.wait_ge(stored, (b * CHUNKS + i) * 16)
                    sp.wait_ge(x_loaded, ((b + 1) * CHUNKS + i - 1) * 16)
                    load(b + 2, i - 1)
                    store(b, i)
                sp.wait_ge(stored, (b + 1) * CHUNKS * 16)
                sp.wait_ge(x_loaded, ((b + 2) * CHUNKS - 1) * 16)
                load(b + 2, CHUNKS - 1)
            with sp.Fori(IMAGES - 2, IMAGES) as b:
                with sp.Fori(0, CHUNKS) as i:
                    store(b, i)
            sp.wait_ge(stored, IMAGES * CHUNKS * 16)

        @block.tensor
        def _(pe):
            mm = nc.tensor.matmul

            def one(dst, lhs, rhs):
                return mm(dst, lhs, rhs, start=True, stop=True)

            def transpose_pieces(dst, src):
                for i in range(PIECES):
                    last = nc.tensor.transpose(dst[:, piece(i)], src[:, piece(i)], ident)
                return last

            pe.wait_ge(weights_loaded, 10 * 16)
            one(bank[0][:, :], whiten[:, :], key_t[:, :])
            one(bank[1][:, 0:C], whiten[:, :], recep_t[:, :]).then_inc(setup_pe, 1)
            pe.wait_ge(setup_dve, 4)
            for j in range(HJ + 1):
                last = one(bank[2][:, j:j + 1], raw_kr[:, piece(j)], b2)
            last.then_inc(setup_pe, 1)

            def group_norm(b, which, part):
                n = norms_before(b, which) * GN_DVE
                if part == 1:
                    pe.wait_ge(gn_dve, n + 1)
                    one(small[:, 0:1], group_mean, gn_mv[:, 0:1]).then_inc(gn_pe, 1)
                if part == 2:
                    pe.wait_ge(gn_dve, n + 5)
                    one(small[:, 1:2], group_mean, gn_tmp[:, 2:3]).then_inc(gn_pe, 1)

            def small_free(b, which, part):
                pe.wait_ge(gn_dve, norms_before(b, which) * GN_DVE + (3 if part == 1 else 6))

            def whole_norm(b, which):
                if which == 1:
                    pe.wait_ge(z_lo_ready, ALL)
                for part in (1, 2):
                    group_norm(b, which, part)
                    small_free(b, which, part)
                pe.wait_ge(setup_dve, SETUP)

            def step(st, ahead_of_it=0):
                def need(sem_, count):
                    st.wait(pe, sem_, count)

                n0, n1, n2, n3, n4, n5 = (st.n(i) for i in range(6))
                norm_part = st.norm[2]

                def product(dst, w):
                    mm(dst, wkr_hi[:, w], z_hi[:, :], start=True, stop=False)
                    mm(dst, wkr_lo[:, w], z_hi[:, :], start=False, stop=False)
                    return mm(dst, wkr_hi[:, w], z_lo[:, :], start=False, stop=True)

                def keys(j):
                    if st.on(4):
                        if j == 0:
                            need(z_lo_ready, n4 + 1)
                        count = n4 * HJ + j - 1
                        if not isinstance(count, int) or count > 0:
                            pe.wait_ge(relu_ready, count)
                        product(bank[3 + j % 2][:, :], piece(j)).then_inc(k_done, 1)

                def values(j):
                    if st.on(5):
                        if j == 0:
                            need(ff_ready, n5)
                        pe.wait_ge(k_ready, n5 * HJ + j + 1)
                        mm(bank[5][:, :], value_t[:, piece(j)], kk[:, j * TILE:(j + 1) * TILE],
                           start=(j == 0), stop=(j == HJ - 1)).then_inc(v_done, 1)

                if ahead_of_it == 1:
                    values(0)
                    values(1)
                    return
                if ahead_of_it == 2:
                    pe.wait_ge(e_ready, st.b * PAIRS)
                    keys(0)
                    values(2)
                    pe.wait_ge(vs_ready, st.b * PAIRS)
                    keys(1)
                    return
                behind = st.behind_layer_1
                if not behind:
                    values(0)
                    values(1)
                else:
                    pe.wait_ge(qs_ready, st.b * PAIRS)
                if st.on(3):
                    need(t1_ready, n3 + 1)
                    need(normed_ready[2], n3)
                    transpose_pieces(bank[2], t1).then_inc(pix_done[2], 1)
                if norm_part == 2:
                    need(z_lo_ready, n3)
                    group_norm(*st.norm)
                if not behind:
                    keys(0)
                else:
                    pe.wait_ge(ys_ready, st.b * TILES)
                if st.on(0):
                    need(gx_ready, n0 + 1)
                    need(normed_ready[0], n0)
                    transpose_pieces(bank[0], gx).then_inc(pix_done[0], 1)
                if not behind:
                    values(2)
                if st.on(2):
                    need(normed_ready[1], n2 + 1)
                    need(t1_ready, n2)
                    transpose_pieces(bank[6], normed[1]).then_inc(back_done[1], 1)
                if st.on(1):
                    need(normed_ready[0], n1 + 1)
                    need(z_lo_ready, n3)
                    if norm_part == 2:
                        small_free(*st.norm)
                    transpose_pieces(bank[7], normed[0]).then_inc(back_done[0], 1)
                if not behind:
                    keys(1)
                values(3)
                if st.on(4):
                    need(silu_ready, n2 + 1)
                    product(bank[6][:, :], piece(HJ)).then_inc(r_done, 1)
                if norm_part == 1:
                    need(t0_ready, n1 + 1)
                    group_norm(*st.norm)
                if st.on(1):
                    need(t0_ready, n1 + 1)
                    need(normed_ready[1], n1)
                    transpose_pieces(bank[1], t0).then_inc(pix_done[1], 1)
                keys(2)
                keys(3)
                if st.on(3):
                    need(normed_ready[2], n3 + 1)
                    need(t0_ready, n1 + 1)
                    if norm_part == 1:
                        small_free(*st.norm)
                    transpose_pieces(bank[7], normed[2]).then_inc(back_done[2], 1)
                if st.on(2):
                    need(silu_ready, n2 + 1)
                    need(tanh_ready, n4 + 1)
                    one(bank[6][:, :], two_out_t[:, :], s[:, :]).then_inc(w_done, 1)

            def layer_1(b):
                all_of_it = isinstance(b, int) and b == IMAGES - 1
                st = Step(IMAGES, LAG - 1) if all_of_it else Step(b + 1, HEAD - 1)

                def need(sem_, count, each=1):
                    pair_wait(pe, sem_, b, count, each)

                def starts(p, lag):
                    return isinstance(p, int) and p == lag

                def project(dst, which):
                    w = qkv_t[:, which * IC:(which + 1) * IC]
                    one(dst[0:IC, :], w, hx[0][:, :])
                    return one(dst[IC:C, :], w, hx[1][:, :])

                for p in pair_steps(pe):
                    ends = p - PAIRS if isinstance(p, int) and not all_of_it else None
                    if pair_on(p, 3) and ends == 2:
                        step(Step(b + 1, HEAD, 0, 0), ahead_of_it=2)
                    if pair_on(p, 1):
                        if starts(p, 1):
                            st.wait(pe, normed_ready[2], st.n(3) + 1)
                            st.wait(pe, z_lo_ready, st.n(3) + 1)
                        need(e_ready, p)
                        need(rec_ready, p - 1)
                        one(den_bank[:, :], exp_b[:, :], e[:, :]).then_inc(den_done, 1)
                        need(qs_ready, p - 1)
                        project(q_bank, 0).then_inc(qb_done, 1)
                    if pair_on(p, 3):
                        if starts(p, 3):
                            st.wait(pe, normed_ready[0], st.n(0) + 1)
                            st.wait(pe, normed_ready[1], st.n(1) + 1)
                        need(o_lo_ready, p - 2)
                        for h in range(2):
                            need(ys_ready, (p - 4) * 2 + h + 1, 2)
                            half = slice(h * IC, (h + 1) * IC)
                            mm(bank[h][:, :], wm_hi[half, :], o_hi[half, :], start=True, stop=False)
                            mm(bank[h][:, :], wm_lo[half, :], o_hi[half, :], start=False, stop=False)
                            mm(bank[h][:, :], wm_hi[half, :], o_lo[half, :], start=False, stop=True)\
                                .then_inc(ob_done, 1)
                    if pair_on(p, 1):
                        if starts(p, 1):
                            st.wait(pe, t1_ready, st.n(2) + 1)
                        need(ev_ready, p)
                        need(ratio_ready, p - 1)
                        one(num_bank[:, :], exp_b[:, :], ev[:, :]).then_inc(num_done, 1)
                    if pair_on(p, 0):
                        if starts(p, 0):
                            pe.wait_ge(relu_ready, (ALL if all_of_it else st.n(4) + 1) * HJ - 1)
                        need(hx_ready, (p + 1) * 2, 2)
                        need(e_ready, p)
                        project(k_bank, 1).then_inc(kb_done, 1)
                        if starts(p, 0):
                            st.wait(pe, relu_ready, st.n(4) + 1, HJ)
                        need(vs_ready, p)
                        project(v_bank, 2).then_inc(vb_done, 1)
                    if ends == 0:
                        step(Step(b + 1, HEAD, 0, 0), ahead_of_it=1)

            run(pe, whole_norm, step, layer_1)

        @block.scalar
        def _(act):
            f = nc.scalar.activation
            act.wait_ge(consts_set, 2)
            act.wait_ge(weights_loaded, 10 * 16)
            for h in range(2):
                q = slice(h * IC, (h + 1) * IC)
                last = f(exp_b[q, q], bt[q, :], ACT.Exp)
            last.then_inc(exp_b_ready, 1)
            act.wait_ge(setup_dve, SETUP)

            def whole_norm(b, which):
                pass

            def norm(st, i, lag):
                if not st.on(lag):
                    return
                st.wait(act, shift_ready[i], st.n(lag) + 1)
                st.wait(act, back_done[i], st.n(lag))
                for q in range(PIECES):
                    last = f(normed[i][:, piece(q)], bank[i][:, piece(q)], ACT.Identity,
                             bias=shift[i][:, q:q + 1], scale=rstd[i][:, q:q + 1])
                last.then_inc(normed_ready[i], 1)

            def shift_x(b, p):
                for h in range(2):
                    f(hx[h][:, :], tile_at(b, p * 2 + h), ACT.Identity, bias=shift_out[:, :],
                      scale=gain_out[:, :]).then_inc(hx_ready, 1)

            def step(st):
                def need(sem_, count, each=1):
                    st.wait(act, sem_, count, each)

                n0, n1, n2, n3, n4 = (st.n(i) for i in range(5))

                def relu(j):
                    if st.on(4):
                        count = (n4 - 1) * HJ + j + 1
                        if not isinstance(count, int) or count > 0:
                            act.wait_ge(v_done, count)
                        act.wait_ge(k_done, n4 * HJ + j + 1)
                        f(kk[:, j * TILE:(j + 1) * TILE], bank[3 + j % 2][:, :], ACT.Relu,
                          bias=bias_kr[:, j:j + 1]).then_inc(relu_ready, 1)

                relu(0)
                if st.on(2):
                    need(back_done[1], n2 + 1)
                    need(w_done, n2)
                    f(s[:, :], bank[6][:, :], ACT.Silu, bias=b1, scale=g1).then_inc(silu_ready, 1)
                if st.on(1):
                    need(back_done[0], n1 + 1)
                    need(pix_done[1], n1)
                    need(t0_kept_ready, n1)
                    f(t0[:, :], bank[7][:, :], ACT.Identity, bias=two_b0, scale=two_g0).then_inc(t0_ready, 1)
                relu(1)
                norm(st, 2, 3)
                if st.on(4):
                    need(r_done, n4 + 1)
                    need(ff_ready, n4)
                    f(th[:, :], bank[6][:, :], ACT.Tanh, bias=half_bias_r[:, :], scale=0.5).then_inc(tanh_ready, 1)
                relu(2)
                if st.on(3):
                    need(back_done[2], n3 + 1)
                    need(k_done, n3, HJ)
                    f(z_hi[:, :], bank[7][:, :], ACT.Copy).then_inc(z_hi_ready, 1)
                if st.starts_layer_1:
                    act.wait_ge(gn_dve, (norms_before(st.b - 1, 1) + 1) * GN_DVE)
                    shift_x(st.b - 1, 0)
                relu(3)
                if not st.starts_layer_1:
                    norm(st, 0, 0)
                    norm(st, 1, 1)

            def layer_1(b):
                last = isinstance(b, int) and b == IMAGES - 1
                if last:
                    act.wait_ge(gn_dve, (norms_before(b, 1) + 1) * GN_DVE)

                def need(sem_, count, each=1):
                    pair_wait(act, sem_, b, count, each)

                for p in pair_steps(act):
                    def copy_y(h, lag):
                        if pair_on(p, lag):
                            need(ob_done, (p - lag) * 2 + h + 1, 2)
                            need(y_ready, (p - lag - 1) * 2 + h + 1, 2)
                            f(ys[h][:, :], bank[h][:, :], ACT.Copy).then_inc(ys_ready, 1)

                    copy_y(1, 4)
                    if pair_on(p, 0) and (last or not isinstance(p, int) or p > 0):
                        need(qb_done, p)
                        shift_x(b, p)
                    copy_y(0, 3)
                    if pair_on(p, 0):
                        need(kb_done, p + 1)
                        need(den_done, p)
                        need(ev_ready, p)
                        f(e[:, :], k_bank[:, :], ACT.Exp).then_inc(e_ready, 1)
                    if pair_on(p, 2):
                        need(o_ready, p - 1)
                        need(ob_done, (p - 2) * 2, 2)
                        f(o_hi[:, :], o[:, :], ACT.Copy).then_inc(o_hi_ready, 1)
                    if pair_on(p, 1):
                        need(qb_done, p)
                        need(o_ready, p - 1)
                        f(qs[:, :], q_bank[:, :], ACT.Copy).then_inc(qs_ready, 1)
                    if pair_on(p, 0):
                        need(vb_done, p + 1)
                        need(ev_ready, p)
                        f(vs[:, :], v_bank[:, :], ACT.Copy).then_inc(vs_ready, 1)
                    if not last and isinstance(p, int) and p < 2:
                        norm(Step(b + 1, HEAD - 1), p, p)

            run(act, whole_norm, step, layer_1)

        @block.gpsimd
        def _(pool):
            tt = nc.gpsimd.tensor_tensor
            nc.gpsimd.memset(minus_half[:, :], -0.5).then_inc(consts_set, 1)
            nc.gpsimd.memset(exp_b[:, :], 0.0).then_inc(consts_set, 1)
            pool.wait_ge(consts_set, 2)

            def whole_norm(b, which):
                pool.wait_ge(gn_dve, norms_before(b, which) * GN_DVE + 6)
                gain = (gain_in, gain_out)[which]
                tt(gain[:, :], gn_tmp[:, 3:4], minus_half[:, 0:1], ALU.pow).then_inc(gn_gain, 1)

            def square(st, j, lag):
                if st.on(lag):
                    pool.wait_ge(relu_ready, st.n(lag) * HJ + j + 1)
                    k = kk[:, j * TILE:(j + 1) * TILE]
                    tt(k, k, k, ALU.mult).then_inc(k_ready, 1)

            def step(st):
                def need(sem_, count):
                    st.wait(pool, sem_, count)

                n3 = st.n(3)

                def rsqrt(i, lag):
                    if st.on(lag):
                        need(var_ready[i], st.n(lag) + 1)
                        need(normed_ready[i], st.n(lag))
                        tt(rstd[i][:, :], var[i][:, :], minus_half[:, :], ALU.pow).then_inc(rstd_ready[i], 1)

                if not st.behind_layer_1:
                    square(st, 3, 5)
                if st.on(3):
                    need(t1_ready, n3 + 1)
                    acc = tile_at(*st.place(3))
                    tt(acc, acc, t1[:, :], ALU.add).then_inc(acc_ready, 1)
                rsqrt(2, 3)
                if st.norm[2] == 2:
                    whole_norm(*st.norm[:2])
                square(st, 0, 4)
                rsqrt(0, 0)
                square(st, 1, 4)
                rsqrt(1, 1)
                square(st, 2, 4)

            def layer_1(b):
                def need(sem_, count, each=1):
                    pair_wait(pool, sem_, b, count, each)

                for p in pair_steps(pool):
                    def add_y(h, lag):
                        if pair_on(p, lag):
                            need(ys_ready, (p - lag) * 2 + h + 1, 2)
                            y = tile_at(b, (p - lag) * 2 + h)
                            tt(y, y, ys[h][:, :], ALU.add).then_inc(y_ready, 1)

                    if pair_on(p, 1):
                        need(vs_ready, p)
                        need(e_ready, p)
                        need(num_done, p - 1)
                        tt(ev[:, :], e[:, :], vs[:, :], ALU.mult).then_inc(ev_ready, 1)
                    if isinstance(p, int) and p == PAIRS + 1 and not (isinstance(b, int) and b == IMAGES - 1):
                        square(Step(b + 1, HEAD), 3, 5)
                    add_y(1, 4)
                    add_y(0, 3)

            run(pool, whole_norm, step, layer_1)

        @block.vector
        def _(dve):
            v = nc.vector

            def first_stats(*chunks):
                for i in chunks:
                    dve.wait_ge(first_loaded[i], 16)
                    for t in range(i * TILES // CHUNKS, (i + 1) * TILES // CHUNKS):
                        v.bn_stats(gn_in[:, t * 6:(t + 1) * 6], xs[:, t * TILE:(t + 1) * TILE]).then_inc(in_stats, 1)

            first_stats(0, 1)
            dve.wait_ge(weights_loaded, 10 * 16)
            v.tensor_scalar(two_out_t[:, :], out_t[:, :], 2.0, None, ALU.mult).then_inc(setup_dve, 1)
            v.tensor_scalar(vec_2[:, :], vec[:, 0:2], 2.0, None, ALU.mult).then_inc(setup_dve, 1)
            first_stats(2)
            dve.wait_ge(setup_pe, 1)
            v.tensor_copy(raw_kr[:, 0:HID], bank[0][:, :]).then_inc(setup_dve, 1)
            v.tensor_copy(raw_kr[:, HID:HID + C], bank[1][:, 0:C]).then_inc(setup_dve, 1)
            dve.wait_ge(setup_dve, 4)
            v.tensor_scalar(wkr[:, :], raw_kr[:, :], g2, None, ALU.mult).then_inc(setup_dve, 1)
            first_stats(3)
            dve.wait_ge(setup_pe, 2)
            v.tensor_copy(bias_kr[:, :], bank[2][:, 0:HJ + 1]).then_inc(setup_dve, 1)
            v.tensor_scalar(half_bias_r[:, :], bank[2][:, HJ:HJ + 1], 0.5, None, ALU.mult).then_inc(setup_dve, 1)
            dve.wait_ge(setup_dve, 5)
            v.tensor_copy(wkr_hi[:, :], wkr[:, :]).then_inc(setup_dve, 1)
            v.tensor_copy(wm_hi[:, :], wm_t[:, :]).then_inc(setup_dve, 1)
            first_stats(4)
            dve.wait_ge(setup_dve, 9)
            v.tensor_tensor(wkr_lo[:, :], wkr[:, :], wkr_hi[:, :], ALU.subtract).then_inc(setup_dve, 1)
            v.tensor_tensor(wm_lo[:, :], wm_t[:, :], wm_hi[:, :], ALU.subtract).then_inc(setup_dve, 1)
            dve.wait_ge(exp_b_ready, 1)
            v.memset(scratch[:, :], 0.0).then_inc(setup_dve, 1)
            first_stats(5, 6, 7)

            def group_norm(b, which, part):
                n = norms_before(b, which)
                stats, gain, shift_ = (gn_in, gain_in, shift_in) if which == 0 else (gn_out, gain_out, shift_out)

                def done(k):
                    dve.wait_ge(gn_dve, n * GN_DVE + k)

                mean, channel_var = gn_mv[:, 0:1], gn_mv[:, 1:2]
                off, off2, about, group_var, group = (gn_tmp[:, i:i + 1] for i in range(5))
                if part == 0:
                    v.bn_aggr(gn_mv[:, :], stats[:, :]).then_inc(gn_dve, 1)
                elif part == 1:
                    dve.wait_ge(gn_pe, n * GN_PE + 1)
                    v.tensor_copy(group, small[:, 0:1]).then_inc(gn_dve, 1)
                    v.tensor_tensor(off, mean, small[:, 0:1], ALU.subtract).then_inc(gn_dve, 1)
                    done(3)
                    v.tensor_tensor(off2, off, off, ALU.mult).then_inc(gn_dve, 1)
                    done(4)
                    v.tensor_tensor(about, channel_var, off2, ALU.add).then_inc(gn_dve, 1)
                elif part == 2:
                    dve.wait_ge(gn_pe, n * GN_PE + 2)
                    v.tensor_scalar(group_var, small[:, 1:2], EPS, None, ALU.add).then_inc(gn_dve, 1)
                else:
                    dve.wait_ge(gn_gain, n + 1)
                    v.scalar_tensor_tensor(out=shift_[:, :], in0=group, scalar=-1.0, in1=gain[:, :],
                                           op0=ALU.mult, op1=ALU.mult).then_inc(gn_dve, 1)
                    done(7)

            def stats_taken(b, which):
                if which == 0:
                    dve.wait_ge(in_stats, (b + 1) * TILES)
                else:
                    dve.wait_ge(x1_stats, (b + 1) * TILES)

            def whole_norm(b, which):
                stats_taken(b, which)
                v.memset(scratch[:, :], 0.0)
                for part in range(4):
                    group_norm(b, which, part)

            def step(st):
                def need(sem_, count, each=1):
                    st.wait(dve, sem_, count, each)

                n0, n1, n2, n3, n4, n5, n6 = (st.n(i) for i in range(7))
                norm_b, norm_which, norm_part = st.norm

                def moments(i, lag, epsilon):
                    if not st.on(lag):
                        return
                    n = st.n(lag)
                    h = halves[i]
                    need(pix_done[i], n + 1)
                    for q in range(PIECES):
                        last = v.bn_stats(h[:, q * 6:(q + 1) * 6], bank[i][:, piece(q)])
                    last.then_inc(halves_ready[i], 1)
                    need(halves_ready[i], n + 1)
                    v.tensor_tensor(apart[:, :], h[:, 1::6], h[:, 4::6], ALU.subtract).then_inc(apart_ready[i], 1)
                    v.tensor_tensor(total[i][:, :], h[:, 1::6], h[:, 4::6], ALU.add)
                    v.scalar_tensor_tensor(out=within[:, :], in0=h[:, 2::6], scalar=C * epsilon, in1=h[:, 5::6],
                                           op0=ALU.add, op1=ALU.add)
                    need(apart_ready[i], n + 1)
                    v.scalar_tensor_tensor(out=between[:, :], in0=apart[:, :], scalar=0.25, in1=apart[:, :],
                                           op0=ALU.mult, op1=ALU.mult).then_inc(between_ready[i], 1)
                    need(between_ready[i], n + 1)
                    v.scalar_tensor_tensor(out=var[i][:, :], in0=within[:, :], scalar=1.0 / C, in1=between[:, :],
                                           op0=ALU.mult, op1=ALU.add).then_inc(var_ready[i], 1)

                def shifts(i, lag):
                    if st.on(lag):
                        need(rstd_ready[i], st.n(lag) + 1)
                        v.scalar_tensor_tensor(out=shift[i][:, :], in0=total[i][:, :], scalar=-0.5,
                                               in1=rstd[i][:, :], op0=ALU.mult, op1=ALU.mult)\
                         .then_inc(shift_ready[i], 1)

                def next_stats(k):
                    t = st.loop * AHEAD + k
                    v.bn_stats(gn_in[:, bass.ds(t * 6, 6)], tile_at(st.b + 1, t)).then_inc(in_stats, 1)

                early = norm_part == 1 and norm_which == 0
                if st.on(6):
                    need(x1_ready, n6 + 1)
                if st.ahead and early:
                    dve.wait_ge(x_loaded, (st.b * CHUNKS + st.loop + 1) * 16)
                if st.on(0):
                    need(pix_done[0], n0)
                    v.tensor_scalar(gx[:, :], tile_at(*st.place(0)), gain_in[:, :], shift_in[:, :],
                                    ALU.mult, ALU.add).then_inc(gx_ready, 1)
                elif st.on(6):
                    v.memset(scratch[:, :], 0.0)
                if st.on(6):
                    slot = st.place(6)[1]
                    v.bn_stats(gn_out[:, bass.ds(slot * 6, 6)], tile_at(*st.place(6))).then_inc(x1_stats, 1)
                if early:
                    next_stats(AHEAD - 1)
                if st.on(2):
                    need(t0_ready, n2 + 1)
                    need(t1_ready, n2)
                    if norm_part == 1:
                        stats_taken(norm_b, norm_which)
                    v.tensor_copy(t0_kept[:, :], t0[:, :]).then_inc(t0_kept_ready, 1)
                if norm_part == 1:
                    group_norm(norm_b, norm_which, 0)
                if norm_part == 2:
                    group_norm(norm_b, norm_which, 2)
                moments(2, 3, 4 * EPS)
                moments(0, 0, EPS)
                if st.ahead:
                    dve.wait_ge(x_loaded, (st.b * CHUNKS + st.loop + 1) * 16)
                shifts(2, 3)
                if st.ahead and not norm_part:
                    next_stats(0 if st.u == 0 else st.u + 1)
                    if st.u == 0:
                        next_stats(1)
                    if st.u == 0 and isinstance(st.t, int) and st.t == TILES - UNROLL:
                        next_stats(2)
                if st.on(5):
                    need(v_done, n5 + 1, HJ)
                    need(tanh_ready, n5 + 1)
                    need(x1_ready, n5)
                    v.scalar_tensor_tensor(out=ff[:, :], in0=th[:, :], scalar=1.0, in1=bank[5][:, :],
                                           op0=ALU.add, op1=ALU.mult).then_inc(ff_ready, 1)
                if norm_part == 1:
                    group_norm(norm_b, norm_which, 1)
                shifts(0, 0)
                moments(1, 1, 4 * EPS)
                if st.on(5):
                    need(ff_ready, n5 + 1)
                    need(acc_ready, n5 + 1)
                    x1 = tile_at(*st.place(5))
                    v.tensor_tensor(x1, x1, ff[:, :], ALU.add).then_inc(x1_ready, 1)
                if st.on(3):
                    need(z_hi_ready, n3 + 1)
                    v.tensor_tensor(z_lo[:, :], bank[7][:, :], z_hi[:, :], ALU.subtract).then_inc(z_lo_ready, 1)
                if st.on(2):
                    need(w_done, n2 + 1)
                    need(t0_kept_ready, n2 + 1)
                    need(pix_done[2], n2)
                    need(acc_ready, n2)
                    v.tensor_tensor(t1[:, :], bank[6][:, :], t0_kept[:, :], ALU.add).then_inc(t1_ready, 1)
                shifts(1, 1)
                if norm_part == 2:
                    group_norm(norm_b, norm_which, 3)

            def layer_1(b):
                def need(sem_, count, each=1):
                    pair_wait(dve, sem_, b, count, each)

                for p in pair_steps(dve):
                    if pair_on(p, 1):
                        need(den_done, p)
                        need(ratio_ready, p - 1)
                        v.reciprocal(rec[:, :], den_bank[:, :]).then_inc(rec_ready, 1)
                    if pair_on(p, 2):
                        need(qs_ready, p - 1)
                        need(ratio_ready, p - 1)
                        need(o_lo_ready, p - 2)
                        v.tensor_tensor(o[:, :], qs[:, :], ratio[:, :], ALU.mult).then_inc(o_ready, 1)
                    if pair_on(p, 1):
                        need(num_done, p)
                        need(rec_ready, p)
                        need(o_ready, p - 1)
                        v.tensor_tensor(ratio[:, :], rec[:, :], num_bank[:, :], ALU.mult).then_inc(ratio_ready, 1)
                    if pair_on(p, 2):
                        need(o_hi_ready, p - 1)
                        v.tensor_tensor(o_lo[:, :], o[:, :], o_hi[:, :], ALU.subtract).then_inc(o_lo_ready, 1)

            run(dve, whole_norm, step, layer_1)


def kernel(**inputs):
    import concourse.bacc as bacc
    from concourse.bass_utils import run_bass_kernel_spmd

    a = {k: np.asarray(v) for k, v in inputs.items()}
    l0, l1 = "L0_conv_", "L1_conv_"

    n = np.arange(C)
    consts = np.concatenate([
        (n[:, None] // GROUP == n[None, :] // GROUP) / GROUP,
        np.eye(C),
    ], axis=1).astype(np.float32)

    arrays = {
        "x": a["x"].reshape(IMAGES, C, PIXELS),
        "consts": consts,
        "vecs": np.stack([a[l0 + v] for v in ("ln0_g", "ln0_b", "ln1_g", "ln1_b", "ln2_g", "ln2_b")], axis=1),
        "w_whiten": a[l0 + "W_whiten"],
        "w_key_t": a[l0 + "W_key"].T,
        "w_recep_t": a[l0 + "W_recep"].T,
        "w_value_t": a[l0 + "W_value"].T,
        "w_out_t": a[l0 + "W_out"].T,
        "w_qkv_t": np.concatenate([a[l1 + w].T for w in ("Wq", "Wk", "Wv")], axis=1),
        "b_t": np.concatenate([a[l1 + "B"].T] * 2, axis=0),
        "w_m_t": np.concatenate([a[l1 + "Wm"].T] * 2, axis=0),
    }
    arrays = {k: np.ascontiguousarray(v) for k, v in arrays.items()}

    nc = bacc.Bacc("TRN2", target_bir_lowering=False, num_devices=1)
    args = [nc.dram_tensor(k, v.shape, mybir.dt.from_np(v.dtype), kind="ExternalInput").ap()
            for k, v in arrays.items()]
    out = nc.dram_tensor("out", (IMAGES, C, PIXELS), F32, kind="ExternalOutput").ap()
    preact_kernel(nc, *args, out)
    r = run_bass_kernel_spmd(nc, [arrays], core_ids=[0])
    return r.results[0]["out"].reshape(IMAGES, C, 128, 128)
```
